# Optimizing a Trainium2 kernel written in Bass

```python
import numpy as np
import jax
import jax.numpy as jnp

def _softmax(x, axis=-1):
    return jax.nn.softmax(x, axis=axis)

def _gelu(x):
    return jax.nn.gelu(x, approximate=True)

def _silu(x):
    return jax.nn.silu(x)

def _sigmoid(x):
    return jax.nn.sigmoid(x)

def _layernorm(x, axis=-1, eps=1e-05):
    m = jnp.mean(x, axis=axis, keepdims=True)
    v = jnp.var(x, axis=axis, keepdims=True)
    return (x - m) / jnp.sqrt(v + eps)

def _scatter_add(tgt, idx, src, axis=0):
    return tgt.at[idx].add(src)

def _segment_sum(src, seg, n):
    return jax.ops.segment_sum(src, seg, n)
kernel_name = 'mk_flamingo_gated_d1_seqx_r4_893e5c'

def setup_inputs(seed: int=0):
    np.random.seed(seed)
    _w = jnp.asarray

    def _rec_inputs():
        import jax
        import jax.numpy as jnp
        _rk = jax.random.key(seed)
        x = -0.000125 + 0.9999 * jax.random.normal(jax.random.fold_in(_rk, 1), (4, 512, 512), jnp.float32)
        _lenS = 512 - jax.random.randint(jax.random.fold_in(_rk, 7), (4,), 0, max(1, 512 // 4) + 1, jnp.int32)
        _lenS2 = 512 - jax.random.randint(jax.random.fold_in(_rk, 8), (4,), 0, max(1, 512 // 4) + 1, jnp.int32)
        itok_BxS_13_99985 = jax.random.randint(jax.random.fold_in(_rk, 11), (4, 512), 13, 99986, jnp.int32)
        _ctx_2048P = jax.random.normal(jax.random.fold_in(_rk, 12), (4, 16, 512), jnp.float32)
        _ctx_2048c = jax.random.dirichlet(jax.random.fold_in(_rk, 512), 0.3 * jnp.ones((16,), jnp.float32), (4, 512))
        _ctx_2048t = jnp.einsum('bsk,bkd->bsd', _ctx_2048c, _ctx_2048P)
        _ctx_2048t = _ctx_2048t * jax.lax.rsqrt(jnp.mean(jnp.square(_ctx_2048t)) + 1e-12) * 0.953939
        ctx_2048 = 6.82029e-06 + 0.0200006 * (_ctx_2048t + 0.3 * jax.random.normal(jax.random.fold_in(_rk, 612), (4, 512, 512), jnp.float32))
        _g = jax.random.normal(jax.random.fold_in(_rk, 9001), (2, 1), jnp.float32)
        _g = jnp.sign(_g) * jnp.maximum(jnp.abs(_g), 1.0) + (_g == 0) * 1.0
        g_xattn = _g[0]
        g_ffn = _g[1]
        return (x, itok_BxS_13_99985, ctx_2048, g_xattn, g_ffn)
    x, itok_BxS_13_99985, ctx_2048, g_xattn, g_ffn = _rec_inputs()

    def _L0_xattn_setup():
        import jax, jax.numpy as jnp
        import numpy as np
        B, S, D = (4, 1024, 512)
        E = 4
        F = 2048 // E
        VOCAB = 25000
        key = jax.random.key(seed)
        k1, k2, k3, k4, k5 = jax.random.split(key, 5)
        hidden_states = jax.random.normal(k1, (B, S, D), dtype=jnp.float32)
        token_ids = jax.random.randint(k2, (B, S), 0, VOCAB, dtype=jnp.int64)
        Wg = jax.random.normal(k3, (E, F, D), dtype=jnp.float32) * 0.02
        Wu = jax.random.normal(k4, (E, F, D), dtype=jnp.float32) * 0.02
        Wd = jax.random.normal(k5, (E, D, F), dtype=jnp.float32) * 0.02
        return {'hidden_states': hidden_states, 'token_ids': token_ids, 'Wg': Wg, 'Wu': Wu, 'Wd': Wd}
    _L0_xattn_all = _L0_xattn_setup()
    _L0_xattn_in = {k: v for k, v in _L0_xattn_all.items() if k in ()}
    del _L0_xattn_all

    def _L0_ffn_setup():
        import jax, jax.numpy as jnp
        import numpy as np
        D_MODEL = 512
        D_FF = 352
        N_EXPERTS = 6
        TOP_K = 2
        B, S = (8, 1024)
        key = jax.random.key(seed)
        ks = jax.random.split(key, 6)
        x = jax.random.normal(ks[0], (B, S, D_MODEL), dtype=jnp.float32)
        W1 = jax.random.normal(ks[1], (N_EXPERTS, D_MODEL, D_FF), dtype=jnp.float32) * 0.02
        b1 = jax.random.normal(ks[2], (N_EXPERTS, D_FF), dtype=jnp.float32) * 0.02
        W2 = jax.random.normal(ks[3], (N_EXPERTS, D_FF, D_MODEL), dtype=jnp.float32) * 0.02
        b2 = jax.random.normal(ks[4], (N_EXPERTS, D_MODEL), dtype=jnp.float32) * 0.02
        gate_W = jax.random.normal(ks[5], (N_EXPERTS, D_MODEL), dtype=jnp.float32) * 0.02
        return {'x': x, 'gate_W': gate_W, 'W1': W1, 'b1': b1, 'W2': W2, 'b2': b2}
    _L0_ffn_all = _L0_ffn_setup()
    _L0_ffn_in = {k: v for k, v in _L0_ffn_all.items() if k in ('gate_W', 'W1', 'b1', 'W2', 'b2')}
    del _L0_ffn_all
    return {'x': x, 'itok_BxS_13_99985': itok_BxS_13_99985, 'ctx_2048': ctx_2048, 'g_xattn': g_xattn, 'g_ffn': g_ffn, 'L0_ffn_gate_W': _L0_ffn_in['gate_W'], 'L0_ffn_W1': _L0_ffn_in['W1'], 'L0_ffn_b1': _L0_ffn_in['b1'], 'L0_ffn_W2': _L0_ffn_in['W2'], 'L0_ffn_b2': _L0_ffn_in['b2']}

def reference(x, itok_BxS_13_99985, ctx_2048, g_xattn, g_ffn, L0_ffn_gate_W, L0_ffn_W1, L0_ffn_b1, L0_ffn_W2, L0_ffn_b2):
    import jax
    import jax.numpy as jnp

    def _L0_xattn_ref(hidden_states, token_ids, Wg, Wu, Wd):
        import jax, jax.numpy as jnp
        import numpy as np
        B, S, D = (4, 1024, 512)
        E = 4
        F = 2048 // E
        VOCAB = 25000
        tokens_per_expert = VOCAB // E
        tid = jnp.clip(token_ids, 0, VOCAB - 1)
        expert_ids = jnp.minimum(tid // tokens_per_expert, E - 1)
        out = jnp.zeros_like(hidden_states)
        for e in range(E):
            g = jax.nn.silu(jnp.einsum('bsd,fd->bsf', hidden_states, Wg[e]))
            u = jnp.einsum('bsd,fd->bsf', hidden_states, Wu[e])
            y = jnp.einsum('bsf,df->bsd', g * u, Wd[e])
            out = jnp.where((expert_ids == e)[..., None], y, out)
        return out

    def _L0_ffn_ref(x, gate_W, W1, b1, W2, b2):
        import jax, jax.numpy as jnp
        import numpy as np
        D_MODEL = 512
        D_FF = 352
        N_EXPERTS = 6
        TOP_K = 2
        B, S = (8, 1024)
        gate_logits = jnp.einsum('bd,ed->be', x.mean(axis=1), gate_W)
        gate_probs = jax.nn.softmax(gate_logits, axis=-1)
        topk_vals, topk_idx = jax.lax.top_k(gate_probs, TOP_K)
        topk_vals = topk_vals / topk_vals.sum(axis=-1, keepdims=True)
        W1g = W1[topk_idx]
        b1g = b1[topk_idx]
        W2g = W2[topk_idx]
        b2g = b2[topk_idx]
        h = jnp.einsum('bsd,bkdf->bksf', x, W1g) + b1g[:, :, None, :]
        h = jax.nn.gelu(h, approximate=False)
        eo = jnp.einsum('bksf,bkfd->bksd', h, W2g) + b2g[:, :, None, :]
        return jnp.einsum('bk,bksd->bsd', topk_vals, eo)
    x = x + jnp.tanh(g_xattn[0]) * _L0_xattn_ref(_layernorm(x, axis=-1), itok_BxS_13_99985, ctx_2048, ctx_2048, ctx_2048)
    x = x + jnp.tanh(g_ffn[0]) * _L0_ffn_ref(_layernorm(x, axis=-1), L0_ffn_gate_W, L0_ffn_W1, L0_ffn_b1, L0_ffn_W2, L0_ffn_b2)
    return x

_drawn_inputs = setup_inputs


def setup_inputs(seed=0):
    import zlib

    import numpy as np

    out = dict(_drawn_inputs(seed))
    spreads = {}
    factors = {'L0_ffn_b1': 8.0, 'L0_ffn_b2': 4.059}
    for name, (base, spread) in spreads.items():
        noise = np.random.default_rng([zlib.crc32(name.encode()), seed]).standard_normal(out[name].shape)
        drawn = base * np.exp(spread * noise) if base else spread * noise
        out[name] = jnp.asarray(drawn.astype(out[name].dtype))
    for name, factor in factors.items():
        out[name] = (out[name] * factor).astype(out[name].dtype)
    return out
```

```python
from contextlib import ExitStack

import concourse.bass as bass
from concourse import mybir

FP32 = mybir.dt.float32
FP32R = mybir.dt.float32r
BF16 = mybir.dt.bfloat16
I32 = mybir.dt.int32
U32 = mybir.dt.uint32
ALU = mybir.AluOpType
ACT = mybir.ActivationFunctionType
AX_X = mybir.AxisListType.X

P = 128
EPS = 1e-5
VOCAB = 25000


def at_least(engine, sem, value):
    if not (isinstance(value, int) and value <= 0):
        engine.wait_ge(sem, value)


def wait_apart(engine, sem, value, counted):
    engine.wait_ge(sem, value)
    if not isinstance(value, int):
        engine.sem_inc(counted, 1)


class Chain:

    def __init__(self, engine, sem, counted):
        self.engine, self.sem, self.counted, self.at = engine, sem, counted, 0

    def sign(self, ins):
        self.at = self.at + 1
        ins.then_inc(self.sem, 1)
        return self.at

    def wait(self, count, apart=False):
        if apart:
            wait_apart(self.engine, self.sem, count, self.counted)
        else:
            self.engine.wait_ge(self.sem, count)

    def run(self, ins, apart=False):
        self.wait(self.sign(ins), apart)


def flamingo_kernel(nc, x, ids, ctx, g_xattn, g_ffn, gate_w, w1, b1, w2, b2, out):
    B, S, D = x.shape
    E = ctx.shape[0]
    F1 = ctx.shape[1]
    NE, _, F2 = w1.shape
    N = B * S
    KD = D // P
    DS = D + 2
    KF1 = F1 // P
    IDC = N // P
    TILES = N // P + E - 1
    RING = 6
    LOOPED = (TILES - RING + 1) // RING * RING
    AHEAD = 4
    TT = S // P
    FC = -(-F2 // P)
    FM = [min(P, F2 - c * P) for c in range(FC)]
    BIAS_ROW = FM[-1]
    W1N = KD * F2
    WN = W1N + FC * D
    EXPERT_IDS = VOCAB // E
    assert F1 == D and BIAS_ROW % 32 == 0 and FM[-1] < P and B >= 2

    x_rows = x.rearrange("b s d -> (b s) d")
    x1_rows = nc.dram_tensor("x1_scratch", [N + TILES * P, DS], FP32, kind="Internal").ap()

    with ExitStack() as stack:
        def sb(name, shape, dt=FP32):
            return stack.enter_context(nc.sbuf_tensor(name, shape, dt))

        def sem(name):
            return stack.enter_context(nc.semaphore(name))

        banks = [stack.enter_context(nc.psum_tensor(f"bank{i}", [P, 512], FP32)) for i in range(8)]
        hT_ps, aT_ps, z_ps, y_ps = banks[0:4]
        t_ps, hid_ps, o_ps = banks[0:2], banks[2:4], banks[4:8]

        ctx_hi = sb("ctx_hi", [P, E * KD * F1], FP32R)
        ctx_lo = sb("ctx_lo", [P, E * KD * F1], FP32R)
        raw_ctx = sb("raw_ctx", [P, E, KF1, D])
        arena = raw_ctx[:, :, :, :].rearrange("p e k d -> p (e k d)")
        X1B = TT * DS
        x1b = arena[:, 0:2 * X1B]
        h2 = arena[:, 2 * X1B:2 * X1B + TT * D]
        act = arena[:, 2 * X1B + TT * D:2 * X1B + TT * D + 2 * S].rearrange("p (c t) -> p c t", t=S)
        h2T_hi = ctx_hi[:, 0:2 * KD * S]
        h2T_lo = ctx_lo[:, 0:2 * KD * S]

        w_raw = [sb(f"w_raw{s}", [P, WN]) for s in range(2)]
        w_hi = [sb(f"w_hi{s}", [P, WN], FP32R) for s in range(2)]
        w_lo = [sb(f"w_lo{s}", [P, WN], FP32R) for s in range(2)]
        b1_rows = sb("b1_rows", [NE, F2])
        b1T = sb("b1T", [P, FC, NE])
        act_last = sb("act_last", [P, S])
        a2_hi = ctx_hi[:, 2 * KD * S:(2 * KD + FC) * S].rearrange("p (c t) -> p c t", t=S)
        a2_lo = ctx_lo[:, 2 * KD * S:(2 * KD + FC) * S].rearrange("p (c t) -> p c t", t=S)

        x_ring = sb("x_ring", [P, RING * DS])
        h = sb("h", [P, D])
        hT_hi = sb("hT_hi", [P, KD, P], FP32R)
        hT_lo = sb("hT_lo", [P, KD, P], FP32R)
        a = sb("a", [P, F1])
        aT_hi = sb("aT_hi", [P, KF1, P], FP32R)
        aT_lo = sb("aT_lo", [P, KF1, P], FP32R)

        col_i = sb("col_i", [P, P], I32)
        col = sb("col", [P, P])
        part_i = sb("part_i", [P, 1], I32)
        part = sb("part", [P, 1])
        ident = sb("ident", [P, P])
        below = sb("below", [P, P])
        ones = sb("ones", [P, P])
        half = sb("half", [P, 1])
        slot_i = sb("slot_i", [P, TILES], I32)
        slot = sb("slot", [P, TILES])
        ids_i = sb("ids_i", [P, IDC], I32)
        ids_f = sb("ids_f", [P, IDC])
        least = sb("least", [P, E + 1, IDC])
        member = sb("member", [P, E, IDC])
        scan = sb("scan", [P, E, IDC])
        rowcnt = sb("rowcnt", [P, E])
        cnt_i = sb("cnt_i", [P, E], I32)
        ntile_i = sb("ntile_i", [P, E], I32)
        ntile = sb("ntile", [P, E])
        ends = sb("ends", [P, E])
        base = sb("base", [P, E])
        cand = sb("cand", [P, E, IDC])
        pos = sb("pos", [P, IDC])
        pos_i = sb("pos_i", [P, IDC], I32)
        pslot_i = sb("pslot_i", [P, IDC], I32)
        ptile_i = sb("ptile_i", [P, IDC], I32)
        pslot = sb("pslot", [P, IDC])
        ptile = sb("ptile", [P, IDC])
        DIGITS = 3
        tile_hot = w_raw[0][:, 0:IDC * DIGITS * TILES // 2].bitcast(BF16).rearrange("p (c g j) -> p c g j", g=DIGITS, j=TILES)
        slot_hot = w_raw[1][:, 0:IDC * P // 2].bitcast(BF16).rearrange("p (c s) -> p c s", s=P)
        col_h = sb("col_h", [P, P], BF16)
        found = sb("found", [P, DIGITS, TILES])
        te = sb("te", [P, TILES])
        te_i = sb("te_i", [P, TILES], I32)
        rows_f = sb("rows_f", [P, TILES])
        put_rows = sb("put_rows", [P, TILES], U32)
        get_rows = sb("get_rows", [P, TILES], U32)
        put_idx = sb("put_idx", [P, RING], U32)
        get_idx = sb("get_idx", [P, RING], U32)
        gates_in = sb("gates_in", [1, 2])
        tg = sb("tg", [P, 2])

        stats1 = sb("stats1", [P, 6])
        mv1 = sb("mv1", [P, 2])
        ve1 = sb("ve1", [P, 1])
        rstd1 = sb("rstd1", [P, 1])
        stats2 = sb("stats2", [P, 6])
        mv2 = sb("mv2", [P, 2])
        eps_row = sb("eps_row", [P, 2])
        warm = sb("warm", [1, 2])
        gw_rows = sb("gw_rows", [NE, D])
        gwT = sb("gwT", [P, KD, NE])
        hsum = sb("hsum", [P, KD])
        logit = sb("logit", [1, NE])
        neg_max = sb("neg_max", [1, 1])
        expo = sb("expo", [1, NE])
        esum = sb("esum", [1, 1])
        einv = sb("einv", [1, 1])
        prob = sb("prob", [1, 8])
        top = sb("top", [1, 8])
        top_idx = sb("top_idx", [1, 8], U32)
        tsum = sb("tsum", [1, 1])
        tinv = sb("tinv", [1, 1])
        mix1 = sb("mix1", [1, 2])
        mix = sb("mix", [P, 2 * 2])

        ids_here, gates_here, gw_here = sem("ids_here"), sem("gates_here"), sem("gw_here")
        ctx_here = [sem(f"ctx_here{e}") for e in range(E)]
        iota_made, ones_made, consts_made = sem("iota_made"), sem("ones_made"), sem("consts_made")
        tables_made = sem("tables_made")
        dve_step, pool_step = sem("dve_step"), sem("pool_step")
        ctxT_done, ctx_hi_done, ctx_lo_done = sem("ctxT_done"), sem("ctx_hi_done"), sem("ctx_lo_done")
        rowcnt_done, counts_done, tile_hot_done = sem("rowcnt_done"), sem("counts_done"), sem("tile_hot_done")
        slot_hot_done, rows_done = sem("slot_hot_done"), sem("rows_done")
        routed, tanh_in, tg_done = sem("routed"), sem("tanh_in"), sem("tg_done")
        gwT_done, gwT_copied = sem("gwT_done"), sem("gwT_copied")
        gathered = [sem(f"gathered{r}") for r in range(RING)]
        scattered = [sem(f"scattered{r}") for r in range(RING)]
        x_ready, ve_ready, rstd_ready = sem("x_ready"), sem("ve_ready"), sem("rstd_ready")
        h_ready, hT_done, hT_hi_done, hT_lo_done = sem("h_ready"), sem("hT_done"), sem("hT_hi_done"), sem("hT_lo_done")
        z_done, silu_done, a_ready = sem("z_done"), sem("silu_done"), sem("a_ready")
        aT_done, aT_hi_done, aT_lo_done = sem("aT_done"), sem("aT_hi_done"), sem("aT_lo_done")
        y_done, y_taken, x1_ready = sem("y_done"), sem("y_taken"), sem("x1_ready")
        x1_here, h2_ready = [sem(f"x1_here{t}") for t in range(TT)], sem("h2_ready")
        h2T_done, h2T_hi_done, h2T_lo_done = sem("h2T_done"), sem("h2T_hi_done"), sem("h2T_lo_done")
        logit_done, neg_max_ready = sem("logit_done"), sem("neg_max_ready")
        expo_done, gate_ready, mix1_ready = sem("expo_done"), sem("gate_ready"), sem("mix1_ready")
        mix_spread, mix_ready = sem("mix_spread"), sem("mix_ready")
        w1_here = [sem(f"w1_here{s}") for s in range(2)]
        w2_here = [sem(f"w2_here{s}") for s in range(2)]
        hi_done = [sem(f"hi_done{s}") for s in range(2)]
        lo_done = [sem(f"lo_done{s}") for s in range(2)]
        hid_done, gelu_done, a2_ready = sem("hid_done"), sem("gelu_done"), sem("a2_ready")
        pair_done, o_done, o_taken, out_stored = sem("pair_done"), sem("o_done"), sem("o_taken"), sem("out_stored")
        pads_made, waited = sem("pads_made"), sem("waited")

        block = stack.enter_context(nc.Block())
        W2_DMAS = 3

        primed = (pair_done, o_taken, out_stored, gelu_done, a2_ready)

        def wait_primed(engine, sem, value):
            engine.wait_ge(sem, value + 1)

        @block.sync
        def _(sp):
            sp.dma_start(ids_i[:, :], ids.rearrange("b s -> (b s)").rearrange("(p c) -> p c", c=IDC)).then_inc(ids_here, 16)
            sp.dma_start(gates_in[:, 0:1], g_xattn.rearrange("(o n) -> o n", o=1)).then_inc(gates_here, 16)
            sp.dma_start(gates_in[:, 1:2], g_ffn.rearrange("(o n) -> o n", o=1)).then_inc(gates_here, 16)
            sp.dma_start(gw_rows[:, :], gate_w).then_inc(gw_here, 16)
            sp.dma_start(b1_rows[:, :], b1).then_inc(gw_here, 16)
            for e in range(E):
                sp.dma_start(raw_ctx[:, e], ctx[e].rearrange("(k p) d -> p k d", p=P)).then_inc(ctx_here[e], 16)

            for counted in primed:
                sp.sem_inc(counted, 1)

            def announce(k, r):
                sp.wait_ge(gathered[r], 16 * k + 16)
                sp.sem_inc(x_ready, 1)

            with sp.Fori(0, TILES // RING) as k:
                for r in range(RING):
                    announce(k, r)
            for r in range(TILES % RING):
                announce(TILES // RING, r)

            def load_x1(b):
                for t in range(TT):
                    sp.dma_start(x1b[:, bass.ds((b % 2) * X1B + t * DS, DS)],
                                 x1_rows[bass.ds(b * S + t * P, P), :]).then_inc(x1_here[t], 16)

            def load_experts(b):
                wait_apart(sp, gate_ready, b + 1, waited)
                full = (FC - 1) * P
                chosen = [sp.value_load(top_idx[0:1, s:s + 1], min_val=0, max_val=NE - 1) for s in range(2)]
                for s, e in enumerate(chosen):
                    if not isinstance(b, int):
                        wait_apart(sp, lo_done[s], 2 * b, waited)
                    raw = w_raw[s]
                    sp.dma_start(raw[:, 0:W1N].rearrange("p (k f) -> p k f", f=F2),
                                 w1[bass.ds(e, 1)].rearrange("o (k p) f -> p (o k) f", p=P)).then_inc(w1_here[s], 16)
                    sp.dma_start(raw[:, W1N:W1N + (FC - 1) * D].rearrange("p (c d) -> p c d", d=D),
                                 w2[bass.ds(e, 1), 0:full].rearrange("o (c p) d -> p (o c) d", p=P)).then_inc(w2_here[s], 16)
                    last = raw[:, W1N + (FC - 1) * D:WN]
                    sp.dma_start(last[0:FM[-1], :], w2[bass.ds(e, 1), full:F2].rearrange("o f d -> (o f) d")).then_inc(w2_here[s], 16)
                    sp.dma_start(last[BIAS_ROW:BIAS_ROW + 1, :], b2[bass.ds(e, 1), :]).then_inc(w2_here[s], 16)

            def store(b):
                for t in range(TT):
                    wait_apart(sp, o_taken, TT * b + t + 2, waited)
                    sp.dma_start(out.rearrange("b s d -> (b s) d")[bass.ds(b * S + t * P, P), :],
                                 x1b[:, bass.ds((b % 2) * X1B + t * DS, D)]).then_inc(out_stored, 16)

            for r in range(RING):
                sp.wait_ge(scattered[r], 16 * len(range(r, TILES, RING)))
            sp.wait_ge(ctxT_done, E * KD)
            sp.wait_ge(rows_done, 1)
            load_x1(0)
            sp.wait_ge(pads_made, 3)
            load_experts(0)
            with sp.Fori(0, B - 1) as b:
                wait_apart(sp, h2_ready, TT * b + TT, waited)
                wait_apart(sp, out_stored, 16 * TT * b + 1, waited)
                load_x1(b + 1)
                load_experts(b + 1)
                store(b)
            store(B - 1)
            wait_primed(sp, out_stored, 16 * TT * B)

        @block.gpsimd
        def _(pool):
            pool.iota(col_i[:, :], [[1, P]], base=0, channel_multiplier=0).then_inc(iota_made, 1)
            pool.iota(part_i[:, :], [[0, 1]], base=0, channel_multiplier=1).then_inc(iota_made, 1)
            pool.iota(slot_i[:, :], [[P, TILES]], base=N, channel_multiplier=1).then_inc(iota_made, 1)
            pool.memset(ones[:, :], 1.0).then_inc(ones_made, 1)
            pool.memset(half[:, :], -0.5).then_inc(pool_step, 1)
            pool.wait_ge(pool_step, 1)
            chain = Chain(pool, pool_step, waited)
            chain.at = 1

            def gather(j, r):
                chain.run(pool.tensor_copy(get_idx[:, r:r + 1], get_rows[:, bass.ds(j, 1)]), apart=True)
                pool.indirect_dma_start(x_ring[:, r * DS:r * DS + D], None, x_rows,
                                        bass.IndirectOffsetOnAxis(get_idx[:, r:r + 1], 0)).then_inc(gathered[r], 16)

            def inverse_root(j):
                pool.wait_ge(ve_ready, j + 1)
                pool.tensor_tensor(rstd1[:, :], ve1[:, :], half[:, 0:1],
                                   ALU.pow).then_inc(rstd_ready, 1)

            def scatter(j, r):
                chain.run(pool.tensor_copy(put_idx[:, r:r + 1], put_rows[:, bass.ds(j, 1)]))
                pool.wait_ge(x1_ready, j + 1)
                deviation = x_ring[:, (r + 1) * DS - 1:(r + 1) * DS]
                chain.run(pool.tensor_tensor(deviation, deviation, half[:, 0:1], ALU.pow), apart=True)
                pool.indirect_dma_start(x1_rows, bass.IndirectOffsetOnAxis(put_idx[:, r:r + 1], 0),
                                        x_ring[:, r * DS:(r + 1) * DS], None).then_inc(scattered[r], 16)

            pool.wait_ge(routed, 2)
            for j in range(RING - 1):
                gather(j, j)
            for j in range(AHEAD):
                inverse_root(j)
            scatter(0, 0)
            inverse_root(AHEAD)
            gather(RING - 1, RING - 1)
            STEPS = 3
            steps = chain.at
            with pool.Fori(0, LOOPED // RING) as k:
                chain.at = steps + k * (STEPS * RING)
                for r in range(1, RING + 1):
                    j = k * RING + r
                    scatter(j, r % RING)
                    pool.wait_ge(scattered[r - 1], 16 * k + 16)
                    gather(j + RING - 1, r - 1)
                    inverse_root(j + AHEAD)
            chain.at = steps + LOOPED // RING * (STEPS * RING)
            for j in range(LOOPED + 1, TILES):
                scatter(j, j % RING)
                if j + RING - 1 < TILES:
                    pool.wait_ge(scattered[(j - 1) % RING], 16 * ((j - 1) // RING) + 16)
                    gather(j + RING - 1, (j - 1) % RING)
                if j + AHEAD < TILES:
                    inverse_root(j + AHEAD)

        @block.vector
        def _(dve):
            chain = Chain(dve, dve_step, waited)
            run = chain.run
            dve.wait_ge(iota_made, 3)
            dve.tensor_copy(part[:, :], part_i[:, :]).then_inc(dve_step, 1)
            chain.at = 1
            run(dve.tensor_copy(col[:, :], col_i[:, :]))
            dve.tensor_scalar(ident[:, :], col[:, :], part[:, 0:1], None, ALU.is_equal).then_inc(consts_made, 1)
            dve.tensor_scalar(below[:, :], col[:, :], part[:, 0:1], None, ALU.is_gt).then_inc(consts_made, 1)
            dve.tensor_copy(col_h[:, :], col[:, :]).then_inc(tables_made, 1)
            dve.memset(eps_row[:, 0:1], 0.0).then_inc(tables_made, 1)
            dve.memset(eps_row[:, 1:2], EPS).then_inc(tables_made, 1)
            dve.tensor_copy(slot[:, :], slot_i[:, :]).then_inc(tables_made, 1)
            dve.memset(least[:, 0, :], 1.0).then_inc(tables_made, 1)
            dve.memset(least[:, E, :], 0.0).then_inc(tables_made, 1)

            dve.wait_ge(ids_here, 16)
            run(dve.tensor_copy(ids_f[:, :], ids_i[:, :]))
            for e in range(1, E):
                dve.tensor_scalar(least[:, e, :], ids_f[:, :], float(e * EXPERT_IDS), None, ALU.is_ge).then_inc(tables_made, 1)
            dve.wait_ge(tables_made, 6 + E - 1)
            run(dve.tensor_tensor(member[:, :, :], least[:, 0:E, :], least[:, 1:E + 1, :], ALU.subtract))
            dve.tensor_reduce(rowcnt[:, :], member[:, :, :], AX_X, ALU.add).then_inc(rowcnt_done, 1)
            dve.wait_ge(ones_made, 1)
            flat = member[:, :, :].rearrange("p e c -> p (e c)")
            run(dve.tensor_tensor_scan(scan[:, :, :].rearrange("p e c -> p (e c)"), ones[:, 0:E * IDC], flat, 0.0,
                                       ALU.mult, ALU.add))
            for s in range(2):
                dve.memset(w_raw[s][BIAS_ROW:P, W1N + (FC - 1) * D:WN], 0.0).then_inc(pads_made, 1)
            dve.memset(prob[:, :], -1.0).then_inc(pads_made, 1)
            dve.wait_ge(counts_done, 1)
            prefix, total = hT_ps[:, 0:E], hT_ps[:, E:2 * E]
            run(dve.tensor_scalar(cnt_i[:, :], total, float(P - 1), None, ALU.add))
            run(dve.tensor_single_scalar(ntile_i[:, :], cnt_i[:, :], P.bit_length() - 1, ALU.logical_shift_right))
            run(dve.tensor_copy(ntile[:, :], ntile_i[:, :]))
            run(dve.tensor_tensor_scan(ends[:, :], ones[:, 0:E], ntile[:, :], 0.0, ALU.mult, ALU.add))
            run(dve.tensor_tensor(base[:, :], ends[:, :], ntile[:, :], ALU.subtract))
            run(dve.tensor_scalar(base[:, :], base[:, :], float(P), -1.0, ALU.mult, ALU.add))
            run(dve.tensor_tensor(base[:, :], base[:, :], prefix, ALU.add))
            run(dve.tensor_tensor(base[:, 1:E], base[:, 1:E], scan[:, 0:E - 1, IDC - 1], ALU.subtract))
            run(dve.tensor_tensor(cand[:, :, :], scan[:, :, :], base[:, :].unsqueeze(2).to_broadcast([P, E, IDC]), ALU.add))
            run(dve.tensor_tensor(cand[:, :, :], cand[:, :, :], member[:, :, :], ALU.mult))
            run(dve.tensor_reduce(pos[:, :], cand[:, :, :].rearrange("p e c -> p c e"), AX_X, ALU.add))
            run(dve.tensor_copy(pos_i[:, :], pos[:, :]))
            run(dve.tensor_single_scalar(pslot_i[:, :], pos_i[:, :], P - 1, ALU.bitwise_and))
            run(dve.tensor_single_scalar(ptile_i[:, :], pos_i[:, :], P.bit_length() - 1, ALU.logical_shift_right))
            run(dve.tensor_copy(pslot[:, :], pslot_i[:, :]))
            run(dve.tensor_copy(ptile[:, :], ptile_i[:, :]))
            for c in range(IDC):
                dve.tensor_scalar(slot_hot[:, c, :], col_h[:, :], pslot[:, c:c + 1], None, ALU.is_equal).then_inc(slot_hot_done, 1)
            ones_part = tile_hot[:, :, 2, :]
            run(dve.tensor_tensor(ones_part, col_h[:, 0:TILES].unsqueeze(1).to_broadcast([P, IDC, TILES]),
                                  ptile[:, :].unsqueeze(2).to_broadcast([P, IDC, TILES]), ALU.is_equal))
            dve.tensor_scalar(tile_hot[:, :, 0, :], ones_part, part[:, 0:1], None, ALU.mult).then_inc(tile_hot_done, 1)
            dve.tensor_tensor(tile_hot[:, :, 1, :], ones_part, col_h[:, 0:IDC].unsqueeze(2).to_broadcast([P, IDC, TILES]),
                              ALU.mult).then_inc(tile_hot_done, 1)
            run(dve.tensor_scalar(te[:, :], col[:, 0:TILES], ends[:, 0:1], None, ALU.is_ge))
            for e in range(1, E - 1):
                run(dve.scalar_tensor_tensor(te[:, :], col[:, 0:TILES], ends[:, e:e + 1], te[:, :], ALU.is_ge, ALU.add))
            run(dve.tensor_copy(te_i[:, :], te[:, :]))
            dve.wait_ge(rows_done, 1)
            run(dve.tensor_copy(found[:, :, :].rearrange("p g j -> p (g j)"), aT_ps[:, 0:DIGITS * TILES]))
            own = chain.sign(dve.tensor_tensor(found[:, 2, :], found[:, 2, :], slot[:, :], ALU.mult))
            run(dve.scalar_tensor_tensor(rows_f[:, :], found[:, 0, :], float(IDC), found[:, 1, :], ALU.mult, ALU.add))
            chain.wait(own)
            run(dve.tensor_tensor(rows_f[:, :], rows_f[:, :], slot[:, :], ALU.add))
            run(dve.tensor_tensor(rows_f[:, :], rows_f[:, :], found[:, 2, :], ALU.subtract))
            dve.tensor_scalar(get_rows[:, :], rows_f[:, :], float(N - 1), None, ALU.min).then_inc(routed, 1)
            dve.tensor_copy(put_rows[:, :], rows_f[:, :]).then_inc(routed, 1)

            def ring_row(j, start, size):
                return x_ring[:, bass.ds((j % RING) * DS + start, size)]

            def rows_statistics(j):
                wait_apart(dve, x_ready, j + 1, waited)
                run(dve.bn_stats(stats1[:, :], ring_row(j, 0, D)), apart=True)
                run(dve.bn_aggr(mv1[:, :], stats1[:, :]))
                dve.tensor_scalar(ve1[:, :], mv1[:, 1:2], EPS, None, ALU.add).then_inc(ve_ready, 1)

            def residual(j):
                dve.wait_ge(y_done, j + 1)
                place = ring_row(j, 0, D)
                dve.scalar_tensor_tensor(place, y_ps[:, :], tg[:, 0:1], place, ALU.mult, ALU.add).then_inc(y_taken, 1)
                wait_apart(dve, y_taken, j + 1, waited)
                run(dve.bn_stats(stats2[:, :], ring_row(j, 0, D)), apart=True)
                run(dve.bn_aggr(mv2[:, :], stats2[:, :]))
                dve.tensor_tensor(ring_row(j, D, 2), mv2[:, :], eps_row[:, :], ALU.add).then_inc(x1_ready, 1)

            def normalise(j):
                dve.wait_ge(rstd_ready, j + 1)
                at_least(dve, hT_done, j)
                dve.tensor_scalar(h[:, :], ring_row(j, 0, D), mv1[:, 0:1], rstd1[:, :],
                                  ALU.subtract, ALU.mult).then_inc(h_ready, 1)

            def h_low(j):
                dve.wait_ge(hT_hi_done, j + 1)
                dve.tensor_tensor(hT_lo[:, :, :].rearrange("p k t -> p (k t)"), hT_ps[:, :],
                                  hT_hi[:, :, :].rearrange("p k t -> p (k t)").bitcast(FP32),
                                  ALU.subtract).then_inc(hT_lo_done, 1)

            def a_low(j):
                dve.wait_ge(aT_hi_done, j + 1)
                dve.tensor_tensor(aT_lo[:, :, :].rearrange("p k t -> p (k t)"), aT_ps[:, :],
                                  aT_hi[:, :, :].rearrange("p k t -> p (k t)").bitcast(FP32),
                                  ALU.subtract).then_inc(aT_lo_done, 1)

            def up(j):
                dve.wait_ge(silu_done, j + 1)
                dve.tensor_tensor(a[:, :], z_ps[:, :], a[:, :], ALU.mult).then_inc(a_ready, 1)

            first_tiles = {6: lambda: rows_statistics(0), 8: lambda: normalise(0),
                           9: lambda: rows_statistics(1), 13: lambda: h_low(0), 14: lambda: normalise(1)}
            for n in range(E * KD):
                first_tiles.get(n, lambda: None)()
                dve.wait_ge(ctx_hi_done, n + 1)
                dve.tensor_tensor(ctx_lo[:, n * F1:(n + 1) * F1], o_ps[n % 4][:, :],
                                  ctx_hi[:, n * F1:(n + 1) * F1].bitcast(FP32), ALU.subtract).then_inc(ctx_lo_done, 1)
                if n == 1:
                    dve.wait_ge(gwT_done, 1)
                    dve.tensor_copy(gwT[:, :, :], y_ps[:, 0:KD * NE].rearrange("p (k e) -> p k e", e=NE)).then_inc(gwT_copied, 1)
                    for c in range(FC):
                        dve.tensor_copy(b1T[0:FM[c], c, :], y_ps[0:FM[c], (KD + c) * NE:(KD + c + 1) * NE]).then_inc(gwT_copied, 1)
            dve.wait_ge(tg_done, 1)
            h_low(1)
            up(0)
            rows_statistics(2)
            dve.memset(act_last[:, :], 1.0).then_inc(pads_made, 1)
            a_low(0)
            normalise(2)
            h_low(2)
            up(1)
            rows_statistics(3)
            STEPS = 4
            steps = chain.at
            with dve.Fori(2, TILES - 2) as j:
                chain.at = steps + (j - 2) * STEPS
                a_low(j - 1)
                normalise(j + 1)
                residual(j - 2)
                h_low(j + 1)
                up(j)
                rows_statistics(j + 2)
            chain.at = steps + (TILES - 4) * STEPS
            a_low(TILES - 3)
            normalise(TILES - 1)
            residual(TILES - 4)
            h_low(TILES - 1)
            up(TILES - 2)
            a_low(TILES - 2)
            residual(TILES - 3)
            up(TILES - 1)
            a_low(TILES - 1)
            residual(TILES - 2)
            residual(TILES - 1)

            def ffn_normalise(b):
                at_least(dve, h2T_done, KD * b)
                for t in range(TT):
                    dve.wait_ge(x1_here[t], 16 * b + 16)
                    at = (b % 2) * X1B + t * DS
                    dve.tensor_scalar(h2[:, t * D:(t + 1) * D], x1b[:, bass.ds(at, D)], x1b[:, bass.ds(at + D, 1)],
                                      x1b[:, bass.ds(at + D + 1, 1)], ALU.subtract, ALU.mult).then_inc(h2_ready, 1)

            def ffn_h_low(b, banks):
                for k in range(KD):
                    dve.wait_ge(h2T_hi_done, KD * b + k + 1)
                    place = bass.ds((b % 2) * (KD * S) + k * S, S)
                    dve.tensor_tensor(h2T_lo[:, place], banks[k % len(banks)][:, :], h2T_hi[:, place].bitcast(FP32),
                                      ALU.subtract).then_inc(h2T_lo_done, 1)

            def choose(b):
                dve.wait_ge(logit_done, b + 1)
                run(dve.tensor_scalar(logit[:, :], t_ps[0][0:1, 0:NE], 1.0 / S, None, ALU.mult))
                dve.tensor_reduce(neg_max[:, :], logit[:, :], AX_X, ALU.max, negate=True).then_inc(neg_max_ready, 1)
                dve.wait_ge(expo_done, b + 1)
                run(dve.reciprocal(einv[:, :], esum[:, :]))
                run(dve.tensor_scalar(prob[:, 0:NE], expo[:, :], einv[:, 0:1], None, ALU.mult), apart=True)
                run(dve.max(top[:, :], prob[:, :]), apart=True)
                dve.max_index(top_idx[:, :], top[:, :], prob[:, :]).then_inc(gate_ready, 1)
                run(dve.tensor_tensor(tsum[:, :], top[:, 0:1], top[:, 1:2], ALU.add))
                run(dve.reciprocal(tinv[:, :], tsum[:, :]))
                dve.tensor_scalar(mix1[:, :], top[:, 0:2], tinv[:, 0:1], tg[0:1, 1:2],
                                  ALU.mult, ALU.mult).then_inc(mix1_ready, 1)

            def spread_mix(b):
                dve.wait_ge(mix_spread, b + 1)
                dve.tensor_copy(mix[:, bass.ds((b % 2) * 2, 2)], t_ps[1][:, 0:2]).then_inc(mix_ready, 1)

            def split_low(b, s, part):
                dve.wait_ge(hi_done[s], 2 * b + part + 1)
                place = slice(0, W1N) if part == 0 else slice(W1N, WN)
                dve.tensor_tensor(w_lo[s][:, place], w_raw[s][:, place], w_hi[s][:, place].bitcast(FP32),
                                  ALU.subtract).then_inc(lo_done[s], 1)

            def weigh(b, s, c):
                dve.wait_ge(gelu_done, (2 * b + s) * FC + c + 2)
                wait_primed(dve, pair_done, 2 * b + s)
                if s == 0 and c == 0:
                    dve.wait_ge(mix_ready, b + 1)
                rows = P if c < FC - 1 else BIAS_ROW + 1
                src = act[0:rows, c % 2, :] if c < FC - 1 else act_last[0:rows, :]
                w = mix[0:rows, bass.ds((b % 2) * 2 + s, 1)]
                run(dve.tensor_scalar(a2_hi[0:rows, c, :], src, w, None, ALU.mult))
                dve.scalar_tensor_tensor(a2_lo[0:rows, c, :], src, w, a2_hi[0:rows, c, :].bitcast(FP32),
                                         ALU.mult, ALU.subtract).then_inc(a2_ready, 1)

            def finish(b):
                for t in range(TT):
                    dve.wait_ge(o_done, TT * b + t + 1)
                    place = x1b[:, bass.ds((b % 2) * X1B + t * DS, D)]
                    dve.tensor_tensor(place, o_ps[t][:, :], place, ALU.add).then_inc(o_taken, 1)

            dve.wait_ge(pads_made, 4)
            ffn_normalise(0)
            ffn_h_low(0, banks[0:KD])
            choose(0)
            split_low(0, 0, 0)
            split_low(0, 0, 1)
            spread_mix(0)
            steps = chain.at
            STEPS_OF_BATCH = 6 + 2 * FC

            def batch(b, more):
                split_low(b, 1, 0)
                weigh(b, 0, 0)
                split_low(b, 1, 1)
                for c in range(1, FC):
                    weigh(b, 0, c)
                if more:
                    ffn_normalise(b + 1)
                    ffn_h_low(b + 1, t_ps)
                weigh(b, 1, 0)
                if more:
                    choose(b + 1)
                for c in range(1, FC):
                    weigh(b, 1, c)
                if more:
                    spread_mix(b + 1)
                    split_low(b + 1, 0, 0)
                    split_low(b + 1, 0, 1)
                finish(b)

            with dve.Fori(0, B - 1) as b:
                chain.at = steps + b * STEPS_OF_BATCH
                batch(b, True)
            chain.at = steps + (B - 1) * STEPS_OF_BATCH
            batch(B - 1, False)

        @block.scalar
        def _(sc):
            sc.wait_ge(tanh_in, 1)
            sc.activation(tg[:, :], z_ps[:, 0:2], ACT.Tanh).then_inc(tg_done, 1)
            def h_high(j):
                sc.wait_ge(hT_done, j + 1)
                at_least(sc, z_done, j)
                sc.activation(hT_hi[:, :, :].rearrange("p k t -> p (k t)"), hT_ps[:, :], ACT.Copy).then_inc(hT_hi_done, 1)

            def a_high(j):
                sc.wait_ge(aT_done, j + 1)
                at_least(sc, y_done, j)
                sc.activation(aT_hi[:, :, :].rearrange("p k t -> p (k t)"), aT_ps[:, :], ACT.Copy).then_inc(aT_hi_done, 1)

            def silu_of(j):
                sc.wait_ge(z_done, j + 1)
                sc.activation(a[:, :], z_ps[:, :], ACT.Silu).then_inc(silu_done, 1)

            sc.wait_ge(tg_done, 1)
            sc.activation(warm[:, :], tg[0:1, :], ACT.Silu)
            for n in range(E * KD):
                if n == 13:
                    h_high(0)
                sc.wait_ge(ctxT_done, n + 1)
                sc.activation(ctx_hi[:, n * F1:(n + 1) * F1], o_ps[n % 4][:, :], ACT.Copy).then_inc(ctx_hi_done, 1)

            silu_of(0)
            h_high(1)
            with sc.Fori(1, TILES - 1) as j:
                a_high(j - 1)
                silu_of(j)
                h_high(j + 1)
            a_high(TILES - 2)
            silu_of(TILES - 1)
            a_high(TILES - 1)

            sc.activation(warm[:, :], tg[0:1, :], ACT.Exp)

            def ffn_h_high(b, banks):
                for k in range(KD):
                    sc.wait_ge(h2T_done, KD * b + k + 1)
                    sc.activation(h2T_hi[:, bass.ds((b % 2) * (KD * S) + k * S, S)], banks[k % len(banks)][:, :],
                                  ACT.Identity, accum_out=hsum[:, k:k + 1]).then_inc(h2T_hi_done, 1)

            def exponents(b):
                sc.wait_ge(neg_max_ready, b + 1)
                sc.activation(expo[:, :], logit[:, :], ACT.Exp, bias=neg_max[:, 0:1],
                              accum_out=esum[:, 0:1]).then_inc(expo_done, 1)

            def split_high(b, s, part):
                here, each = (w1_here[s], 16) if part == 0 else (w2_here[s], 16 * W2_DMAS)
                sc.wait_ge(here, each * (b + 1))
                if not (isinstance(b, int) and b == 0 and s == 0):
                    wait_primed(sc, pair_done, 2 * b + s - 1)
                place = slice(0, W1N) if part == 0 else slice(W1N, WN)
                sc.activation(w_hi[s][:, place], w_raw[s][:, place], ACT.Copy).then_inc(hi_done[s], 1)

            def gelu_of(b, s, c, e):
                k = s * FC + c
                sc.wait_ge(hid_done, 2 * FC * b + k + 1)
                rows = FM[c]
                dst = act[:, c % 2, :] if c < FC - 1 else act_last[0:rows, :]
                wait_primed(sc, a2_ready, 2 * FC * b + max(k - FC + 1, 0))
                sc.activation(dst, hid_ps[k % 2][0:rows, :], ACT.Gelu, bias=b1T[0:rows, c, bass.ds(e, 1)]).then_inc(gelu_done, 1)

            sc.wait_ge(gwT_copied, 1 + FC)
            ffn_h_high(0, banks[0:KD])
            exponents(0)
            split_high(0, 0, 0)
            split_high(0, 0, 1)

            def batch(b, more):
                wait_apart(sc, gate_ready, b + 1, waited)
                chosen = [sc.value_load(top_idx[0:1, s:s + 1], min_val=0, max_val=NE - 1) for s in range(2)]
                split_high(b, 1, 0)
                split_high(b, 1, 1)
                for c in range(FC):
                    gelu_of(b, 0, c, chosen[0])
                if more:
                    ffn_h_high(b + 1, t_ps)
                gelu_of(b, 1, 0, chosen[1])
                if more:
                    exponents(b + 1)
                for c in range(1, FC):
                    gelu_of(b, 1, c, chosen[1])
                if more:
                    split_high(b + 1, 0, 0)
                    split_high(b + 1, 0, 1)

            with sc.Fori(0, B - 1) as b:
                batch(b, True)
            batch(B - 1, False)

        @block.tensor
        def _(pe):
            pe.wait_ge(consts_made, 2)
            pe.wait_ge(ones_made, 1)
            pe.wait_ge(gates_here, 32)
            pe.matmul(z_ps[:, 0:2], ones[0:1, :], gates_in[0:1, :], start=True, stop=True).then_inc(tanh_in, 1)
            pe.wait_ge(rowcnt_done, 1)
            pe.matmul(hT_ps[:, 0:E], below[:, :], rowcnt[:, :], start=True, stop=True)
            pe.matmul(hT_ps[:, E:2 * E], ones[:, :], rowcnt[:, :], start=True, stop=True).then_inc(counts_done, 1)
            pe.wait_ge(gw_here, 32)
            for k in range(KD):
                last = pe.matmul(y_ps[:, k * NE:(k + 1) * NE], gw_rows[:, k * P:(k + 1) * P], ident[0:NE, 0:NE],
                                 start=True, stop=True)
            for c in range(FC):
                last = pe.matmul(y_ps[0:FM[c], (KD + c) * NE:(KD + c + 1) * NE], b1_rows[:, c * P:c * P + FM[c]],
                                 ident[0:NE, 0:NE], start=True, stop=True)
            last.then_inc(gwT_done, 1)
            def invert():
                pe.wait_ge(slot_hot_done, IDC)
                pe.wait_ge(tile_hot_done, 2)
                for c in range(IDC):
                    last = pe.matmul(aT_ps[:, 0:DIGITS * TILES], slot_hot[:, c, :],
                                     tile_hot[:, c].rearrange("p g j -> p (g j)"), start=(c == 0), stop=(c == IDC - 1))
                last.then_inc(rows_done, 1)

            def split_product(dst, stationary, moving, first, last):
                s_hi, s_lo = stationary
                m_hi, m_lo = moving
                pe.matmul(dst, s_hi, m_lo, start=first, stop=False)
                pe.matmul(dst, s_hi, m_hi, start=False, stop=False)
                return pe.matmul(dst, s_lo, m_hi, start=False, stop=last)

            def transpose_h(j):
                pe.wait_ge(h_ready, j + 1)
                at_least(pe, hT_lo_done, j)
                for k in range(KD):
                    last = pe.transpose(hT_ps[:, k * P:(k + 1) * P], h[:, k * P:(k + 1) * P], ident[:, :])
                last.then_inc(hT_done, 1)

            def transpose_a(j):
                pe.wait_ge(a_ready, j + 1)
                at_least(pe, aT_lo_done, j)
                for k in range(KF1):
                    last = pe.transpose(aT_ps[:, k * P:(k + 1) * P], a[:, k * P:(k + 1) * P], ident[:, :])
                last.then_inc(aT_done, 1)

            def expert_product(j, dst, src_hi, src_lo):
                e = pe.value_load(te_i[0:1, bass.ds(j, 1)], min_val=0, max_val=E - 1)
                for k in range(KD):
                    place = bass.ds(e * (KD * F1) + k * F1, F1)
                    last = split_product(dst[:, :], (src_hi[:, k, :], src_lo[:, k, :]), (ctx_hi[:, place], ctx_lo[:, place]),
                                         k == 0, k == KD - 1)
                return last

            def first_product(j):
                pe.wait_ge(hT_lo_done, j + 1)
                at_least(pe, a_ready, j)
                expert_product(j, z_ps, hT_hi, hT_lo).then_inc(z_done, 1)

            def second_product(j):
                pe.wait_ge(aT_lo_done, j + 1)
                at_least(pe, y_taken, j)
                expert_product(j, y_ps, aT_hi, aT_lo).then_inc(y_done, 1)

            for n in range(E * KD):
                if n == 4:
                    invert()
                if n == 13:
                    transpose_h(0)
                e, k = divmod(n, KD)
                if k == 0:
                    pe.wait_ge(ctx_here[e], 16)
                if n >= 4:
                    pe.wait_ge(ctx_lo_done, n - 3)
                for m in range(KF1):
                    last = pe.transpose(o_ps[n % 4][:, m * P:(m + 1) * P], raw_ctx[:, e, m, k * P:(k + 1) * P], ident[:, :])
                last.then_inc(ctxT_done, 1)

            pe.wait_ge(ctx_lo_done, E * KD)
            pe.wait_ge(routed, 2)
            pe.wait_ge(tg_done, 1)
            pe.wait_ge(gwT_copied, 1 + FC)
            first_product(0)
            transpose_h(1)
            with pe.Fori(1, TILES - 1) as j:
                transpose_a(j - 1)
                first_product(j)
                transpose_h(j + 1)
                second_product(j - 1)
            transpose_a(TILES - 2)
            first_product(TILES - 1)
            second_product(TILES - 2)
            transpose_a(TILES - 1)
            second_product(TILES - 1)

            def transpose_h2(b, ks):
                pe.wait_ge(h2_ready, TT * b + TT)
                for k in ks:
                    if k == 1:
                        pe.wait_ge(mix_ready, b)
                    pe.wait_ge(h2T_lo_done, KD * b + max(k - 1, 0))
                    for t in range(TT):
                        last = pe.transpose(t_ps[k % 2][:, t * P:(t + 1) * P],
                                            h2[:, t * D + k * P:t * D + (k + 1) * P], ident[:, :])
                    last.then_inc(h2T_done, 1)

            def transpose_first_h2():
                for t in range(TT):
                    pe.wait_ge(h2_ready, t + 1)
                    for k in range(KD):
                        last = pe.transpose(banks[k][:, t * P:(t + 1) * P],
                                            h2[:, t * D + k * P:t * D + (k + 1) * P], ident[:, :])
                        if t == TT - 1:
                            last.then_inc(h2T_done, 1)

            def logits(b):
                pe.wait_ge(h2T_lo_done, KD * b + KD)
                for k in range(KD):
                    last = pe.matmul(t_ps[0][0:1, 0:NE], hsum[:, k:k + 1], gwT[:, k, :], start=(k == 0), stop=(k == KD - 1))
                last.then_inc(logit_done, 1)

            def spread_mix(b):
                pe.wait_ge(mix1_ready, b + 1)
                pe.matmul(t_ps[1][:, 0:2], ones[0:1, :], mix1[:, :], start=True, stop=True).then_inc(mix_spread, 1)

            def hidden(b, s, between=()):
                pe.wait_ge(lo_done[s], 2 * b + 1)
                pe.wait_ge(h2T_lo_done, KD * b + KD)
                for c in range(FC):
                    k6 = s * FC + c
                    wait_primed(pe, gelu_done, 2 * FC * b + max(k6 - 1, 0))
                    for k in range(KD):
                        col0 = k * F2 + c * P
                        rows = bass.ds((b % 2) * (KD * S) + k * S, S)
                        last = split_product(hid_ps[k6 % 2][0:FM[c], :],
                                             (w_hi[s][:, col0:col0 + FM[c]], w_lo[s][:, col0:col0 + FM[c]]),
                                             (h2T_hi[:, rows], h2T_lo[:, rows]), k == 0, k == KD - 1)
                    last.then_inc(hid_done, 1)
                    if c < len(between):
                        between[c](b + 1)

            def output(b, s, cs):
                pe.wait_ge(lo_done[s], 2 * b + 2)
                for c in cs:
                    pe.wait_ge(a2_ready, (2 * b + s) * FC + c + 2)
                if s == 0 and cs[0] == 0:
                    wait_primed(pe, o_taken, TT * b)
                for t in range(TT):
                    for c in cs:
                        rows = P if c < FC - 1 else BIAS_ROW + 1
                        place = slice(W1N + c * D, W1N + (c + 1) * D)
                        last = split_product(o_ps[t][:, :],
                                             (a2_hi[0:rows, c, t * P:(t + 1) * P], a2_lo[0:rows, c, t * P:(t + 1) * P]),
                                             (w_hi[s][0:rows, place], w_lo[s][0:rows, place]),
                                             s == 0 and c == 0, s == 1 and c == FC - 1)
                    if s == 1 and cs[-1] == FC - 1:
                        last.then_inc(o_done, 1)
                return last

            transpose_first_h2()
            logits(0)
            spread_mix(0)
            full = list(range(FC - 1))

            def batch(b, more):
                hidden(b, 0)
                output(b, 0, full)
                if more:
                    transpose_h2(b + 1, (0, 1))
                output(b, 0, [FC - 1]).then_inc(pair_done, 1)
                if more:
                    transpose_h2(b + 1, (2, 3))
                hidden(b, 1, (logits, spread_mix) if more else ())
                output(b, 1, full)
                output(b, 1, [FC - 1])
                pe.drain().then_inc(pair_done, 1)

            with pe.Fori(0, B - 1) as b:
                batch(b, True)
            batch(B - 1, False)


_INS = ["x", "itok_BxS_13_99985", "ctx_2048", "g_xattn", "g_ffn", "L0_ffn_gate_W", "L0_ffn_W1", "L0_ffn_b1",
        "L0_ffn_W2", "L0_ffn_b2"]


def kernel(**inputs):
    import numpy as _np
    import concourse.bacc as _bacc
    from concourse import mybir as _mybir
    from concourse.bass_utils import run_bass_kernel_spmd as _run

    nc = _bacc.Bacc("TRN2", target_bir_lowering=False, num_devices=1)
    arrays, args = {}, []
    for name in _INS:
        a = _np.ascontiguousarray(inputs[name])
        arrays[f"in_{name}"] = a
        args.append(nc.dram_tensor(f"in_{name}", a.shape, _mybir.dt.from_np(a.dtype), kind="ExternalInput").ap())
    shape = inputs["x"].shape
    args.append(nc.dram_tensor("out_0", shape, _mybir.dt.float32, kind="ExternalOutput").ap())
    flamingo_kernel(nc, *args)
    r = _run(nc, [arrays], core_ids=[0])
    return r.results[0]["out_0"]
```

```python
from contextlib import ExitStack

import concourse.bass as bass
from concourse import mybir

FP32 = mybir.dt.float32
FP32R = mybir.dt.float32r
BF16 = mybir.dt.bfloat16
I32 = mybir.dt.int32
U32 = mybir.dt.uint32
ALU = mybir.AluOpType
ACT = mybir.ActivationFunctionType
AX_X = mybir.AxisListType.X

P = 128
EPS = 1e-5
VOCAB = 25000


def at_least(engine, sem, value):
    if not (isinstance(value, int) and value <= 0):
        engine.wait_ge(sem, value)


def wait_apart(engine, sem, value, counted):
    engine.wait_ge(sem, value)
    if not isinstance(value, int):
        engine.sem_inc(counted, 1)


class Chain:

    def __init__(self, engine, sem, counted):
        self.engine, self.sem, self.counted, self.at = engine, sem, counted, 0

    def sign(self, ins):
        self.at = self.at + 1
        ins.then_inc(self.sem, 1)
        return self.at

    def wait(self, count, apart=False):
        if apart:
            wait_apart(self.engine, self.sem, count, self.counted)
        else:
            self.engine.wait_ge(self.sem, count)

    def run(self, ins, apart=False):
        self.wait(self.sign(ins), apart)


def flamingo_kernel(nc, x, ids, ctx, g_xattn, g_ffn, gate_w, w1, b1, w2, b2, out):
    B, S, D = x.shape
    E = ctx.shape[0]
    F1 = ctx.shape[1]
    NE, _, F2 = w1.shape
    N = B * S
    KD = D // P
    DS = D + 2
    KF1 = F1 // P
    IDC = N // P
    IDC_BY_POOL = IDC // 4
    TILES = N // P + E - 1
    RING = 6
    LOOPED = (TILES - RING + 1) // RING * RING
    AHEAD = 4
    TT = S // P
    EARLY = TT + E - 1
    PREP = TILES - 7
    BY_ACT = 4
    FC = -(-F2 // P)
    FM = [min(P, F2 - c * P) for c in range(FC)]
    BIAS_ROW = FM[-1]
    W1N = KD * F2
    WN = W1N + FC * D
    PARTS = [slice(0, KD * P), slice(KD * P, W1N), slice(W1N, WN)]
    EXPERT_IDS = VOCAB // E
    assert EARLY < RING + 2 and TILES - 7 > EARLY + 2 and F1 == D and BIAS_ROW % 32 == 0 and FM[-1] < P and B >= 2

    x_rows = x.rearrange("b s d -> (b s) d")
    x1_rows = nc.dram_tensor("x1_scratch", [N + TILES * P, DS], FP32, kind="Internal").ap()

    with ExitStack() as stack:
        def sb(name, shape, dt=FP32):
            return stack.enter_context(nc.sbuf_tensor(name, shape, dt))

        def sem(name):
            return stack.enter_context(nc.semaphore(name))

        banks = [stack.enter_context(nc.psum_tensor(f"bank{i}", [P, 512], FP32)) for i in range(8)]
        hT_ps, aT_ps, z_ps, y_ps = banks[0:4]
        t_ps, hid_ps, o_ps = banks[0:2], banks[2:4], banks[4:8]

        ctx_hi = sb("ctx_hi", [P, E * KD * F1], FP32R)
        ctx_lo = sb("ctx_lo", [P, E * KD * F1], FP32R)
        raw_ctx = sb("raw_ctx", [P, E, KF1, D])
        arena = raw_ctx[:, :, :, :].rearrange("p e k d -> p (e k d)")
        X1B = TT * DS
        x1b = arena[:, 0:2 * X1B]
        h2 = arena[:, 2 * X1B:2 * X1B + TT * D]
        act = arena[:, 2 * X1B + TT * D:2 * X1B + TT * D + 2 * S].rearrange("p (c t) -> p c t", t=S)
        h2T_hi = ctx_hi[:, 0:2 * KD * S]
        h2T_lo = ctx_lo[:, 0:2 * KD * S]

        w_raw = [sb(f"w_raw{s}", [P, WN]) for s in range(2)]
        w_hi = [sb(f"w_hi{s}", [P, WN], FP32R) for s in range(2)]
        w_lo = [sb(f"w_lo{s}", [P, WN], FP32R) for s in range(2)]
        b1_rows = sb("b1_rows", [NE, F2])
        b1T = sb("b1T", [P, FC, NE])
        act_last = sb("act_last", [P, S])
        a2_hi = ctx_hi[:, 2 * KD * S:(2 * KD + FC) * S].rearrange("p (c t) -> p c t", t=S)
        a2_lo = ctx_lo[:, 2 * KD * S:(2 * KD + FC) * S].rearrange("p (c t) -> p c t", t=S)

        x_ring = sb("x_ring", [P, RING * DS])
        h = sb("h", [P, D])
        hT_hi = sb("hT_hi", [P, KD, P], FP32R)
        hT_lo = sb("hT_lo", [P, KD, P], FP32R)
        a = sb("a", [P, F1])
        aT_hi = sb("aT_hi", [P, KF1, P], FP32R)
        aT_lo = sb("aT_lo", [P, KF1, P], FP32R)

        col_i = sb("col_i", [P, P], I32)
        col = sb("col", [P, P])
        part_i = sb("part_i", [P, 1], I32)
        part = sb("part", [P, 1])
        ident = sb("ident", [P, P])
        neg_ident = sb("neg_ident", [P, P], FP32R)
        below = sb("below", [P, P])
        early = sb("early", [P, P])
        ones = sb("ones", [P, P])
        half = sb("half", [P, 1])
        slot_i = sb("slot_i", [P, TILES], I32)
        slot = sb("slot", [P, TILES])
        ids_i = sb("ids_i", [P, IDC], I32)
        ids_f = sb("ids_f", [P, IDC])
        least = sb("least", [P, E + 1, IDC])
        member = sb("member", [P, E, IDC])
        scan = sb("scan", [P, E, IDC])
        rowcnt = sb("rowcnt", [P, E])
        cnt_i = sb("cnt_i", [P, 2 * E], I32)
        ntile_i = sb("ntile_i", [P, 2 * E], I32)
        ntile = sb("ntile", [P, 2 * E])
        ends = sb("ends", [P, 2 * E])
        starts = sb("starts", [P, 2 * E])
        shift = sb("shift", [P, E])
        bound = sb("bound", [P, E])
        base = sb("base", [P, E])
        cand = sb("cand", [P, E, IDC])
        later = sb("later", [P, E, IDC])
        pos = sb("pos", [P, IDC])
        pos_i = sb("pos_i", [P, IDC], I32)
        pslot_i = sb("pslot_i", [P, IDC], I32)
        ptile_i = sb("ptile_i", [P, IDC], I32)
        pslot = sb("pslot", [P, IDC])
        ptile = sb("ptile", [P, IDC])
        DIGITS = 3
        tile_hot = w_raw[0][:, 0:IDC * DIGITS * TILES // 2].bitcast(BF16).rearrange("p (c g j) -> p c g j", g=DIGITS, j=TILES)
        slot_hot = w_raw[1][:, 0:IDC * P // 2].bitcast(BF16).rearrange("p (c s) -> p c s", s=P)
        col_h = sb("col_h", [P, P], BF16)
        found = sb("found", [P, DIGITS, TILES])
        te = sb("te", [P, TILES])
        te_i = sb("te_i", [P, TILES], I32)
        rows_f = sb("rows_f", [P, TILES])
        put_rows = sb("put_rows", [P, TILES], U32)
        get_rows = sb("get_rows", [P, TILES], U32)
        put_idx = sb("put_idx", [P, RING], U32)
        get_idx = sb("get_idx", [P, RING], U32)
        gates_in = sb("gates_in", [1, 2])
        tg = sb("tg", [P, 2])

        stats1 = sb("stats1", [P, 6])
        mv1 = sb("mv1", [P, 2])
        ve1 = sb("ve1", [P, 1])
        rstd1 = sb("rstd1", [P, 1])
        stats2 = sb("stats2", [P, 6])
        mv2 = sb("mv2", [P, 2])
        eps_row = sb("eps_row", [P, 2])
        warm = sb("warm", [1, 2])
        gw_rows = sb("gw_rows", [NE, D])
        gwT = sb("gwT", [P, KD, NE])
        hsum = sb("hsum", [P, KD])
        logit = sb("logit", [1, NE])
        neg_max = sb("neg_max", [1, 1])
        expo = sb("expo", [1, NE])
        esum = sb("esum", [1, 1])
        einv = sb("einv", [1, 1])
        prob = sb("prob", [1, 8])
        top = sb("top", [1, 8])
        top_idx = sb("top_idx", [1, 8], U32)
        tsum = sb("tsum", [1, 1])
        tinv = sb("tinv", [1, 1])
        mix1 = sb("mix1", [1, 2])
        mix = sb("mix", [P, 2 * 2])

        ids_here, gates_here, gw_here = sem("ids_here"), sem("gates_here"), sem("gw_here")
        ctx_here = [sem(f"ctx_here{e}") for e in range(E)]
        iota_made, ones_made, consts_made = sem("iota_made"), sem("ones_made"), sem("consts_made")
        tables_made = sem("tables_made")
        dve_step, pool_step = sem("dve_step"), sem("pool_step")
        ctxT_done, ctx_hi_done, ctx_lo_done = sem("ctxT_done"), sem("ctx_hi_done"), sem("ctx_lo_done")
        rowcnt_done, counts_done, tile_hot_done = sem("rowcnt_done"), sem("counts_done"), sem("tile_hot_done")
        pslot_done = sem("pslot_done")
        slot_hot_done, rows_done = sem("slot_hot_done"), sem("rows_done")
        routed, tanh_in, tg_done = sem("routed"), sem("tanh_in"), sem("tg_done")
        gwT_done, gwT_copied = sem("gwT_done"), sem("gwT_copied")
        gathered = [sem(f"gathered{r}") for r in range(RING)]
        scattered = [sem(f"scattered{r}") for r in range(RING)]
        x_ready, ve_ready, rstd_ready = sem("x_ready"), sem("ve_ready"), sem("rstd_ready")
        h_ready, hT_done, hT_hi_done, hT_lo_done = sem("h_ready"), sem("hT_done"), sem("hT_hi_done"), sem("hT_lo_done")
        z_done, silu_done, a_ready = sem("z_done"), sem("silu_done"), sem("a_ready")
        aT_done, aT_hi_done, aT_lo_done = sem("aT_done"), sem("aT_hi_done"), sem("aT_lo_done")
        y_done, y_taken, x1_ready = sem("y_done"), sem("y_taken"), sem("x1_ready")
        x1_here, h2_ready = [sem(f"x1_here{t}") for t in range(TT)], sem("h2_ready")
        h2T_done, h2T_hi_done, h2T_lo_done = sem("h2T_done"), sem("h2T_hi_done"), sem("h2T_lo_done")
        logit_done, neg_max_ready = sem("logit_done"), sem("neg_max_ready")
        expo_done, gate_ready, mix1_ready = sem("expo_done"), sem("gate_ready"), sem("mix1_ready")
        mix_spread, mix_ready = sem("mix_spread"), sem("mix_ready")
        w1_here = [sem(f"w1_here{s}") for s in range(2)]
        w1_rest_here = [sem(f"w1_rest_here{s}") for s in range(2)]
        w2_here = [sem(f"w2_here{s}") for s in range(2)]
        hi_done = [sem(f"hi_done{s}") for s in range(2)]
        lo_done = [sem(f"lo_done{s}") for s in range(2)]
        hid_done, gelu_done, a2_ready = sem("hid_done"), sem("gelu_done"), sem("a2_ready")
        pair_done, o_done, o_taken, out_stored = sem("pair_done"), sem("o_done"), sem("o_taken"), sem("out_stored")
        pads_made, waited = sem("pads_made"), sem("waited")
        tiles_landed, warmed, sums_done = sem("tiles_landed"), sem("warmed"), sem("sums_done")
        ctx_rest_done, ctx_lo_by_act = sem("ctx_rest_done"), sem("ctx_lo_by_act")

        block = stack.enter_context(nc.Block())
        W2_DMAS = 3

        primed = (pair_done, o_taken, out_stored, gelu_done, a2_ready)

        def wait_primed(engine, sem, value):
            engine.wait_ge(sem, value + 1)

        @block.sync
        def _(sp):
            sp.dma_start(ids_i[:, :], ids.rearrange("b s -> (b s)").rearrange("(p c) -> p c", c=IDC)).then_inc(ids_here, 16)
            sp.dma_start(gates_in[:, 0:1], g_xattn.rearrange("(o n) -> o n", o=1)).then_inc(gates_here, 16)
            sp.dma_start(gates_in[:, 1:2], g_ffn.rearrange("(o n) -> o n", o=1)).then_inc(gates_here, 16)
            sp.dma_start(gw_rows[:, :], gate_w).then_inc(gw_here, 16)
            sp.dma_start(b1_rows[:, :], b1).then_inc(gw_here, 16)
            for e in range(E):
                sp.dma_start(raw_ctx[:, e], ctx[e].rearrange("(k p) d -> p k d", p=P)).then_inc(ctx_here[e], 16)

            for counted in primed:
                sp.sem_inc(counted, 1)

            def announce(k, r):
                sp.wait_ge(gathered[r], 16 * k + 16)
                sp.sem_inc(x_ready, 1)

            with sp.Fori(0, PREP // RING) as k:
                for r in range(RING):
                    announce(k, r)

            def load_x1(b):
                for t in range(TT):
                    sp.dma_start(x1b[:, bass.ds((b % 2) * X1B + t * DS, DS)],
                                 x1_rows[bass.ds(b * S + t * P, P), :]).then_inc(x1_here[t], 16)

            def load_experts(b):
                wait_apart(sp, gate_ready, b + 1, waited)
                full = (FC - 1) * P
                chosen = [sp.value_load(top_idx[0:1, s:s + 1], min_val=0, max_val=NE - 1) for s in range(2)]
                for s, e in enumerate(chosen):
                    if not isinstance(b, int):
                        wait_apart(sp, lo_done[s], len(PARTS) * b, waited)
                    raw = w_raw[s]
                    for place, width in ((PARTS[0], slice(0, P)), (PARTS[1], slice(P, F2))):
                        sp.dma_start(raw[:, place].rearrange("p (k f) -> p k f", k=KD),
                                     w1[bass.ds(e, 1), :, width].rearrange("o (k p) f -> p (o k) f", p=P)
                                     ).then_inc((w1_here if width.start == 0 else w1_rest_here)[s], 16)
                    sp.dma_start(raw[:, W1N:W1N + (FC - 1) * D].rearrange("p (c d) -> p c d", d=D),
                                 w2[bass.ds(e, 1), 0:full].rearrange("o (c p) d -> p (o c) d", p=P)).then_inc(w2_here[s], 16)
                    last = raw[:, W1N + (FC - 1) * D:WN]
                    sp.dma_start(last[0:FM[-1], :], w2[bass.ds(e, 1), full:F2].rearrange("o f d -> (o f) d")).then_inc(w2_here[s], 16)
                    sp.dma_start(last[BIAS_ROW:BIAS_ROW + 1, :], b2[bass.ds(e, 1), :]).then_inc(w2_here[s], 16)

            def store(b):
                for t in range(TT):
                    wait_apart(sp, o_taken, TT * b + t + 2, waited)
                    sp.dma_start(out.rearrange("b s d -> (b s) d")[bass.ds(b * S + t * P, P), :],
                                 x1b[:, bass.ds((b % 2) * X1B + t * DS, D)]).then_inc(out_stored, 16)

            sp.wait_ge(ctxT_done, E * KD)
            sp.wait_ge(tiles_landed, EARLY)
            load_x1(0)
            for j in range(PREP // RING * RING, TILES):
                announce(j // RING, j % RING)
            sp.wait_ge(rows_done, 1)
            sp.wait_ge(pads_made, 3)
            load_experts(0)
            sp.wait_ge(tiles_landed, TILES)
            with sp.Fori(0, B - 1) as b:
                wait_apart(sp, h2_ready, TT * b + TT, waited)
                wait_apart(sp, out_stored, 16 * TT * b + 1, waited)
                load_x1(b + 1)
                load_experts(b + 1)
                store(b)
            store(B - 1)
            wait_primed(sp, out_stored, 16 * TT * B)

        @block.gpsimd
        def _(pool):
            pool.iota(col_i[:, :], [[1, P]], base=0, channel_multiplier=0).then_inc(iota_made, 1)
            pool.iota(part_i[:, :], [[0, 1]], base=0, channel_multiplier=1).then_inc(iota_made, 1)
            pool.iota(slot_i[:, :], [[P, TILES]], base=N, channel_multiplier=1).then_inc(iota_made, 1)
            pool.memset(ones[:, :], 1.0).then_inc(ones_made, 1)
            pool.memset(half[:, :], -0.5).then_inc(pool_step, 1)
            pool.wait_ge(pool_step, 1)
            chain = Chain(pool, pool_step, waited)
            chain.at = 1

            pool.wait_ge(pslot_done, 1)
            for c in range(IDC_BY_POOL):
                pool.tensor_scalar(slot_hot[:, c, :], col_h[:, :], pslot[:, c:c + 1], None, ALU.is_equal).then_inc(slot_hot_done, 1)

            def gather(j, r):
                chain.run(pool.tensor_copy(get_idx[:, r:r + 1], get_rows[:, bass.ds(j, 1)]), apart=True)
                pool.indirect_dma_start(x_ring[:, r * DS:r * DS + D], None, x_rows,
                                        bass.IndirectOffsetOnAxis(get_idx[:, r:r + 1], 0)).then_inc(gathered[r], 16)

            def inverse_root(j):
                pool.wait_ge(ve_ready, j + 1)
                pool.tensor_tensor(rstd1[:, :], ve1[:, :], half[:, 0:1],
                                   ALU.pow).then_inc(rstd_ready, 1)

            def scatter(j, r):
                chain.run(pool.tensor_copy(put_idx[:, r:r + 1], put_rows[:, bass.ds(j, 1)]))
                pool.wait_ge(x1_ready, j + 1)
                deviation = x_ring[:, (r + 1) * DS - 1:(r + 1) * DS]
                chain.run(pool.tensor_tensor(deviation, deviation, half[:, 0:1], ALU.pow), apart=True)
                pool.indirect_dma_start(x1_rows, bass.IndirectOffsetOnAxis(put_idx[:, r:r + 1], 0),
                                        x_ring[:, r * DS:(r + 1) * DS], None).then_inc(scattered[r], 16)

            def landed(j):
                pool.wait_ge(scattered[j % RING], 16 * (j // RING) + 16)
                pool.sem_inc(tiles_landed, 1)

            pool.wait_ge(routed, 2)
            for j in range(RING - 1):
                gather(j, j)
                if j >= 2:
                    inverse_root(j - 2)
            inverse_root(RING - 3)
            scatter(0, 0)
            inverse_root(AHEAD)
            gather(RING - 1, RING - 1)
            STEPS = 3
            steps = chain.at
            with pool.Fori(0, LOOPED // RING) as k:
                chain.at = steps + k * (STEPS * RING)
                for r in range(1, RING + 1):
                    j = k * RING + r
                    scatter(j, r % RING)
                    pool.wait_ge(scattered[r - 1], 16 * k + 16)
                    pool.sem_inc(tiles_landed, 1)
                    gather(j + RING - 1, r - 1)
                    inverse_root(j + AHEAD)
            chain.at = steps + LOOPED // RING * (STEPS * RING)
            for j in range(LOOPED + 1, TILES):
                scatter(j, j % RING)
                landed(j - 1)
                if j + RING - 1 < TILES:
                    gather(j + RING - 1, (j - 1) % RING)
                if j + AHEAD < TILES:
                    inverse_root(j + AHEAD)
            landed(TILES - 1)

        @block.vector
        def _(dve):
            chain = Chain(dve, dve_step, waited)
            run = chain.run
            dve.wait_ge(iota_made, 3)
            dve.tensor_copy(part[:, :], part_i[:, :]).then_inc(dve_step, 1)
            chain.at = 1
            run(dve.tensor_copy(col[:, :], col_i[:, :]))
            dve.tensor_scalar(ident[:, :], col[:, :], part[:, 0:1], None, ALU.is_equal).then_inc(consts_made, 1)
            dve.tensor_scalar(below[:, :], col[:, :], part[:, 0:1], None, ALU.is_gt).then_inc(consts_made, 1)
            dve.tensor_scalar(neg_ident[:, :], col[:, :], part[:, 0:1], -1.0, ALU.is_equal, ALU.mult).then_inc(consts_made, 1)
            dve.wait_ge(ones_made, 1)
            dve.tensor_scalar(early[:, :], ones[:, :], part[:, 0:1], float(S // IDC), ALU.mult, ALU.is_lt).then_inc(consts_made, 1)
            dve.tensor_copy(col_h[:, :], col[:, :]).then_inc(tables_made, 1)
            dve.memset(eps_row[:, 0:1], 0.0).then_inc(tables_made, 1)
            dve.memset(eps_row[:, 1:2], EPS).then_inc(tables_made, 1)
            dve.tensor_copy(slot[:, :], slot_i[:, :]).then_inc(tables_made, 1)
            dve.memset(least[:, 0, :], 1.0).then_inc(tables_made, 1)
            dve.memset(least[:, E, :], 0.0).then_inc(tables_made, 1)

            dve.wait_ge(ids_here, 16)
            run(dve.tensor_copy(ids_f[:, :], ids_i[:, :]))
            for e in range(1, E):
                dve.tensor_scalar(least[:, e, :], ids_f[:, :], float(e * EXPERT_IDS), None, ALU.is_ge).then_inc(tables_made, 1)
            dve.wait_ge(tables_made, 6 + E - 1)
            run(dve.tensor_tensor(member[:, :, :], least[:, 0:E, :], least[:, 1:E + 1, :], ALU.subtract))
            dve.tensor_reduce(rowcnt[:, :], member[:, :, :], AX_X, ALU.add).then_inc(rowcnt_done, 1)
            flat = member[:, :, :].rearrange("p e c -> p (e c)")
            run(dve.tensor_tensor_scan(scan[:, :, :].rearrange("p e c -> p (e c)"), ones[:, 0:E * IDC], flat, 0.0,
                                       ALU.mult, ALU.add))
            for s in range(2):
                dve.memset(w_raw[s][BIAS_ROW:P, W1N + (FC - 1) * D:WN], 0.0).then_inc(pads_made, 1)
            dve.memset(prob[:, :], -1.0).then_inc(pads_made, 1)
            dve.wait_ge(counts_done, 1)
            prefix, counts = hT_ps[:, 0:E], hT_ps[:, E:3 * E]
            run(dve.tensor_scalar(cnt_i[:, :], counts, float(P - 1), None, ALU.add))
            run(dve.tensor_single_scalar(ntile_i[:, :], cnt_i[:, :], P.bit_length() - 1, ALU.logical_shift_right))
            run(dve.tensor_copy(ntile[:, :], ntile_i[:, :]))
            run(dve.tensor_tensor(ntile[:, E:2 * E], ntile[:, E:2 * E], ntile[:, 0:E], ALU.subtract))
            run(dve.tensor_tensor_scan(ends[:, :], ones[:, 0:2 * E], ntile[:, :], 0.0, ALU.mult, ALU.add))
            run(dve.tensor_tensor(starts[:, :], ends[:, :], ntile[:, :], ALU.subtract))
            run(dve.tensor_scalar(base[:, :], starts[:, 0:E], float(P), -1.0, ALU.mult, ALU.add))
            run(dve.tensor_tensor(base[:, :], base[:, :], prefix, ALU.add))
            based = chain.sign(dve.tensor_tensor(base[:, 1:E], base[:, 1:E], scan[:, 0:E - 1, IDC - 1], ALU.subtract))
            dve.tensor_scalar(bound[:, :], ends[:, 0:E], float(P), None, ALU.mult).then_inc(dve_step, 1)
            chain.at = chain.at + 1
            shifted = chain.sign(dve.tensor_tensor(shift[:, :], starts[:, E:2 * E], ends[:, 0:E], ALU.subtract))
            chain.wait(based)

            def by_expert(values):
                return values.unsqueeze(2).to_broadcast([P, E, IDC])

            run(dve.tensor_tensor(cand[:, :, :], scan[:, :, :], by_expert(base[:, :]), ALU.add))
            chain.wait(shifted)
            run(dve.tensor_tensor(later[:, :, :], cand[:, :, :], by_expert(bound[:, :]), ALU.is_ge))
            run(dve.tensor_tensor(later[:, :, :], later[:, :, :], by_expert(shift[:, :]), ALU.mult))
            run(dve.scalar_tensor_tensor(cand[:, :, :], later[:, :, :], float(P), cand[:, :, :], ALU.mult, ALU.add))
            run(dve.tensor_tensor(cand[:, :, :], cand[:, :, :], member[:, :, :], ALU.mult))
            run(dve.tensor_reduce(pos[:, :], cand[:, :, :].rearrange("p e c -> p c e"), AX_X, ALU.add))
            run(dve.tensor_copy(pos_i[:, :], pos[:, :]))
            run(dve.tensor_single_scalar(pslot_i[:, :], pos_i[:, :], P - 1, ALU.bitwise_and))
            run(dve.tensor_single_scalar(ptile_i[:, :], pos_i[:, :], P.bit_length() - 1, ALU.logical_shift_right))
            dve.tensor_copy(pslot[:, :], pslot_i[:, :]).then_inc(pslot_done, 1)
            run(dve.tensor_copy(ptile[:, :], ptile_i[:, :]))
            dve.wait_ge(pslot_done, 1)
            for c in range(IDC_BY_POOL, IDC):
                dve.tensor_scalar(slot_hot[:, c, :], col_h[:, :], pslot[:, c:c + 1], None, ALU.is_equal).then_inc(slot_hot_done, 1)
            ones_part = tile_hot[:, :, 2, :]
            run(dve.tensor_tensor(ones_part, col_h[:, 0:TILES].unsqueeze(1).to_broadcast([P, IDC, TILES]),
                                  ptile[:, :].unsqueeze(2).to_broadcast([P, IDC, TILES]), ALU.is_equal))
            dve.tensor_scalar(tile_hot[:, :, 0, :], ones_part, part[:, 0:1], None, ALU.mult).then_inc(tile_hot_done, 1)
            dve.tensor_tensor(tile_hot[:, :, 1, :], ones_part, col_h[:, 0:IDC].unsqueeze(2).to_broadcast([P, IDC, TILES]),
                              ALU.mult).then_inc(tile_hot_done, 1)
            run(dve.tensor_scalar(te[:, :], col[:, 0:TILES], ends[:, E - 1:E], -float(E - 1), ALU.is_ge, ALU.mult))
            for e in range(2 * E - 1):
                if e != E - 1:
                    run(dve.scalar_tensor_tensor(te[:, :], col[:, 0:TILES], ends[:, e:e + 1], te[:, :], ALU.is_ge, ALU.add))
            run(dve.tensor_copy(te_i[:, :], te[:, :]))
            dve.wait_ge(rows_done, 1)
            run(dve.tensor_copy(found[:, :, :].rearrange("p g j -> p (g j)"), aT_ps[:, 0:DIGITS * TILES]))
            own = chain.sign(dve.tensor_tensor(found[:, 2, :], found[:, 2, :], slot[:, :], ALU.mult))
            run(dve.scalar_tensor_tensor(rows_f[:, :], found[:, 0, :], float(IDC), found[:, 1, :], ALU.mult, ALU.add))
            chain.wait(own)
            run(dve.tensor_tensor(rows_f[:, :], rows_f[:, :], slot[:, :], ALU.add))
            run(dve.tensor_tensor(rows_f[:, :], rows_f[:, :], found[:, 2, :], ALU.subtract))
            dve.tensor_scalar(get_rows[:, :], rows_f[:, :], float(N - 1), None, ALU.min).then_inc(routed, 1)
            dve.tensor_copy(put_rows[:, :], rows_f[:, :]).then_inc(routed, 1)

            def ring_row(j, start, size):
                return x_ring[:, bass.ds((j % RING) * DS + start, size)]

            def rows_statistics(j):
                wait_apart(dve, x_ready, j + 1, waited)
                run(dve.bn_stats(stats1[:, :], ring_row(j, 0, D)), apart=True)
                run(dve.bn_aggr(mv1[:, :], stats1[:, :]))
                dve.tensor_scalar(ve1[:, :], mv1[:, 1:2], EPS, None, ALU.add).then_inc(ve_ready, 1)

            def residual(j, bank=y_ps):
                dve.wait_ge(y_done, j + 1)
                place = ring_row(j, 0, D)
                dve.scalar_tensor_tensor(place, bank[:, :], tg[:, 0:1], place, ALU.mult, ALU.add).then_inc(y_taken, 1)
                wait_apart(dve, y_taken, j + 1, waited)
                run(dve.bn_stats(stats2[:, :], ring_row(j, 0, D)), apart=True)
                run(dve.bn_aggr(mv2[:, :], stats2[:, :]))
                dve.tensor_tensor(ring_row(j, D, 2), mv2[:, :], eps_row[:, :], ALU.add).then_inc(x1_ready, 1)

            def normalise(j):
                dve.wait_ge(rstd_ready, j + 1)
                at_least(dve, hT_done, j)
                dve.tensor_scalar(h[:, :], ring_row(j, 0, D), mv1[:, 0:1], rstd1[:, :],
                                  ALU.subtract, ALU.mult).then_inc(h_ready, 1)

            def h_low(j):
                dve.wait_ge(hT_hi_done, j + 1)
                dve.tensor_tensor(hT_lo[:, :, :].rearrange("p k t -> p (k t)"), hT_ps[:, :],
                                  hT_hi[:, :, :].rearrange("p k t -> p (k t)").bitcast(FP32),
                                  ALU.subtract).then_inc(hT_lo_done, 1)

            def a_low(j, bank=aT_ps, hi=aT_hi, lo=aT_lo):
                dve.wait_ge(aT_hi_done, j + 1)
                dve.tensor_tensor(lo[:, :, :].rearrange("p k t -> p (k t)"), bank[:, :],
                                  hi[:, :, :].rearrange("p k t -> p (k t)").bitcast(FP32),
                                  ALU.subtract).then_inc(aT_lo_done, 1)

            def up(j):
                dve.wait_ge(silu_done, j + 1)
                dve.tensor_tensor(a[:, :], z_ps[:, :], a[:, :], ALU.mult).then_inc(a_ready, 1)

            first_tiles = {8: lambda: rows_statistics(0), 11: lambda: normalise(0),
                           12: lambda: rows_statistics(1)}
            for n in range(BY_ACT, E * KD):
                first_tiles.get(n, lambda: None)()
                dve.wait_ge(ctx_hi_done, n + 1)
                dve.tensor_tensor(ctx_lo[:, n * F1:(n + 1) * F1], o_ps[n % 4][:, :],
                                  ctx_hi[:, n * F1:(n + 1) * F1].bitcast(FP32), ALU.subtract).then_inc(ctx_lo_done, 1)
                if n == BY_ACT:
                    dve.wait_ge(gwT_done, 1)
                    dve.tensor_copy(gwT[:, :, :], y_ps[:, 0:KD * NE].rearrange("p (k e) -> p k e", e=NE)).then_inc(gwT_copied, 1)
                    for c in range(FC):
                        dve.tensor_copy(b1T[0:FM[c], c, :], y_ps[0:FM[c], (KD + c) * NE:(KD + c + 1) * NE]).then_inc(gwT_copied, 1)
            dve.wait_ge(tg_done, 1)
            h_low(0)
            normalise(1)
            h_low(1)
            up(0)
            rows_statistics(2)
            dve.memset(act_last[:, :], 1.0).then_inc(pads_made, 1)
            a_low(0)
            normalise(2)
            h_low(2)
            up(1)
            rows_statistics(3)
            STEPS = 4
            steps = chain.at
            with dve.Fori(2, PREP) as j:
                chain.at = steps + (j - 2) * STEPS
                a_low(j - 1)
                normalise(j + 1)
                residual(j - 2)
                h_low(j + 1)
                up(j)
                rows_statistics(j + 2)
            chain.at = steps + (PREP - 2) * STEPS
            def ffn_normalise(b, ts=range(TT)):
                at_least(dve, h2T_done, KD * b)
                for t in ts:
                    dve.wait_ge(x1_here[t], 16 * b + 16)
                    at = (b % 2) * X1B + t * DS
                    dve.tensor_scalar(h2[:, t * D:(t + 1) * D], x1b[:, bass.ds(at, D)], x1b[:, bass.ds(at + D, 1)],
                                      x1b[:, bass.ds(at + D + 1, 1)], ALU.subtract, ALU.mult).then_inc(h2_ready, 1)

            def ffn_h_low(b, banks):
                for k in range(KD):
                    dve.wait_ge(h2T_hi_done, KD * b + k + 1)
                    place = bass.ds((b % 2) * (KD * S) + k * S, S)
                    dve.tensor_tensor(h2T_lo[:, place], banks[k % len(banks)][:, :], h2T_hi[:, place].bitcast(FP32),
                                      ALU.subtract).then_inc(h2T_lo_done, 1)

            def scale_logits(b):
                dve.wait_ge(logit_done, b + 1)
                run(dve.tensor_scalar(logit[:, :], t_ps[0][0:1, 0:NE], 1.0 / S, None, ALU.mult))
                dve.tensor_reduce(neg_max[:, :], logit[:, :], AX_X, ALU.max, negate=True).then_inc(neg_max_ready, 1)

            def choose(b):
                dve.wait_ge(expo_done, b + 1)
                run(dve.reciprocal(einv[:, :], esum[:, :]))
                run(dve.tensor_scalar(prob[:, 0:NE], expo[:, :], einv[:, 0:1], None, ALU.mult), apart=True)
                run(dve.max(top[:, :], prob[:, :]), apart=True)
                dve.max_index(top_idx[:, :], top[:, :], prob[:, :]).then_inc(gate_ready, 1)
                run(dve.tensor_tensor(tsum[:, :], top[:, 0:1], top[:, 1:2], ALU.add))
                run(dve.reciprocal(tinv[:, :], tsum[:, :]))
                dve.tensor_scalar(mix1[:, :], top[:, 0:2], tinv[:, 0:1], tg[0:1, 1:2],
                                  ALU.mult, ALU.mult).then_inc(mix1_ready, 1)

            def spread_mix(b):
                dve.wait_ge(mix_spread, b + 1)
                dve.tensor_copy(mix[:, bass.ds((b % 2) * 2, 2)], t_ps[1][:, 0:2]).then_inc(mix_ready, 1)

            def split_low(b, s, piece):
                dve.wait_ge(hi_done[s], len(PARTS) * b + piece + 1)
                place = PARTS[piece]
                dve.tensor_tensor(w_lo[s][:, place], w_raw[s][:, place], w_hi[s][:, place].bitcast(FP32),
                                  ALU.subtract).then_inc(lo_done[s], 1)

            def weigh(b, s, c):
                dve.wait_ge(gelu_done, (2 * b + s) * FC + c + 2)
                wait_primed(dve, pair_done, 2 * b + s)
                if s == 0 and c == 0:
                    dve.wait_ge(mix_ready, b + 1)
                rows = P if c < FC - 1 else BIAS_ROW + 1
                src = act[0:rows, c % 2, :] if c < FC - 1 else act_last[0:rows, :]
                w = mix[0:rows, bass.ds((b % 2) * 2 + s, 1)]
                run(dve.tensor_scalar(a2_hi[0:rows, c, :], src, w, None, ALU.mult))
                dve.scalar_tensor_tensor(a2_lo[0:rows, c, :], src, w, a2_hi[0:rows, c, :].bitcast(FP32),
                                         ALU.mult, ALU.subtract).then_inc(a2_ready, 1)

            def finish(b):
                for t in range(TT):
                    dve.wait_ge(o_done, TT * b + t + 1)
                    place = x1b[:, bass.ds((b % 2) * X1B + t * DS, D)]
                    dve.tensor_tensor(place, o_ps[t][:, :], place, ALU.add).then_inc(o_taken, 1)

            for j in range(PREP, TILES):
                if j == PREP + 5:
                    spread_mix(0)
                a_low(j - 1)
                if j == PREP + 3:
                    scale_logits(0)
                if j + 1 < TILES:
                    normalise(j + 1)
                residual(j - 2)
                if j + 1 < TILES:
                    h_low(j + 1)
                up(j)
                if j + 2 < TILES:
                    rows_statistics(j + 2)
                if j < PREP + 2:
                    half_of_batch = TT // 2 * (j - PREP)
                    ffn_normalise(0, range(half_of_batch, half_of_batch + TT // 2))
                if j == PREP + 3:
                    choose(0)
                if j == PREP + 5:
                    split_low(0, 0, 0)
                    split_low(0, 0, 1)
            a_low(TILES - 1, hT_ps, hT_hi, hT_lo)
            residual(TILES - 2)
            ffn_h_low(0, o_ps)
            residual(TILES - 1, aT_ps)
            dve.wait_ge(pads_made, 4)
            split_low(0, 0, 2)
            steps = chain.at
            STEPS_OF_BATCH = 6 + 2 * FC

            def batch(b, more):
                weigh(b, 0, 0)
                split_low(b, 1, 0)
                split_low(b, 1, 1)
                for c in range(1, FC):
                    weigh(b, 0, c)
                split_low(b, 1, 2)
                if more:
                    ffn_normalise(b + 1)
                    ffn_h_low(b + 1, t_ps)
                    scale_logits(b + 1)
                    choose(b + 1)
                for c in range(FC):
                    weigh(b, 1, c)
                if more:
                    spread_mix(b + 1)
                    for piece in range(len(PARTS)):
                        split_low(b + 1, 0, piece)
                finish(b)

            with dve.Fori(0, B - 1) as b:
                chain.at = steps + b * STEPS_OF_BATCH
                batch(b, True)
            chain.at = steps + (B - 1) * STEPS_OF_BATCH
            batch(B - 1, False)

        @block.scalar
        def _(sc):
            sc.wait_ge(tanh_in, 1)
            sc.activation(tg[:, :], z_ps[:, 0:2], ACT.Tanh).then_inc(tg_done, 1)
            def h_high(j):
                sc.wait_ge(hT_done, j + 1)
                at_least(sc, z_done, j)
                sc.activation(hT_hi[:, :, :].rearrange("p k t -> p (k t)"), hT_ps[:, :], ACT.Copy).then_inc(hT_hi_done, 1)

            def a_high(j):
                sc.wait_ge(aT_done, j + 1)
                at_least(sc, y_done, j)
                sc.activation(aT_hi[:, :, :].rearrange("p k t -> p (k t)"), aT_ps[:, :], ACT.Copy).then_inc(aT_hi_done, 1)

            def silu_of(j):
                sc.wait_ge(z_done, j + 1)
                sc.activation(a[:, :], z_ps[:, :], ACT.Silu).then_inc(silu_done, 1)

            sc.wait_ge(tg_done, 1)
            warming = Chain(sc, warmed, waited)

            def bring_tables(function):
                warming.run(sc.activation(warm[:, :], tg[0:1, :], function))

            bring_tables(ACT.Silu)
            def split_low_alone(n):
                sc.wait_ge(ctx_rest_done, n + 1)
                sc.activation(ctx_lo[:, n * F1:(n + 1) * F1], o_ps[n % 4][:, :], ACT.Copy).then_inc(ctx_lo_by_act, 1)

            for n in range(E * KD):
                sc.wait_ge(ctxT_done, n + 1)
                sc.activation(ctx_hi[:, n * F1:(n + 1) * F1], o_ps[n % 4][:, :], ACT.Copy).then_inc(ctx_hi_done, 1)
                if 1 <= n <= BY_ACT:
                    split_low_alone(n - 1)

            h_high(0)
            silu_of(0)
            h_high(1)
            with sc.Fori(1, PREP) as j:
                a_high(j - 1)
                silu_of(j)
                h_high(j + 1)
            def ffn_h_high(b, banks):
                for k in range(KD):
                    sc.wait_ge(h2T_done, KD * b + k + 1)
                    sc.activation(h2T_hi[:, bass.ds((b % 2) * (KD * S) + k * S, S)], banks[k % len(banks)][:, :],
                                  ACT.Identity, accum_out=hsum[:, k:k + 1]).then_inc(h2T_hi_done, 1)

            def token_sums():
                for k in range(KD):
                    sc.wait_ge(h2T_done, k + 1)
                    sc.activation(x1b[:, X1B + k * S:X1B + (k + 1) * S], o_ps[k][:, :], ACT.Identity,
                                  accum_out=hsum[:, k:k + 1]).then_inc(sums_done, 1)

            def exponents(b):
                sc.wait_ge(neg_max_ready, b + 1)
                sc.activation(expo[:, :], logit[:, :], ACT.Exp, bias=neg_max[:, 0:1],
                              accum_out=esum[:, 0:1]).then_inc(expo_done, 1)

            def split_high(b, s, piece):
                here, each = ((w1_here[s], 16), (w1_rest_here[s], 16), (w2_here[s], 16 * W2_DMAS))[piece]
                sc.wait_ge(here, each * (b + 1))
                if not (isinstance(b, int) and b == 0 and s == 0):
                    wait_primed(sc, pair_done, 2 * b + s - 1)
                place = PARTS[piece]
                sc.activation(w_hi[s][:, place], w_raw[s][:, place], ACT.Copy).then_inc(hi_done[s], 1)

            def gelu_of(b, s, c, e):
                k = s * FC + c
                sc.wait_ge(hid_done, 2 * FC * b + k + 1)
                rows = FM[c]
                dst = act[:, c % 2, :] if c < FC - 1 else act_last[0:rows, :]
                wait_primed(sc, a2_ready, 2 * FC * b + max(k - FC + 1, 0))
                sc.activation(dst, hid_ps[k % 2][0:rows, :], ACT.Gelu, bias=b1T[0:rows, c, bass.ds(e, 1)]).then_inc(gelu_done, 1)

            for j in range(PREP, TILES):
                a_high(j - 1)
                silu_of(j)
                if j + 1 < TILES:
                    h_high(j + 1)
                if j == PREP + 2:
                    token_sums()
                if j == PREP + 3:
                    exponents(0)
                    bring_tables(ACT.Silu)
                if j == PREP + 5:
                    split_high(0, 0, 0)
                    split_high(0, 0, 1)
            sc.wait_ge(aT_done, TILES)
            sc.activation(hT_hi[:, :, :].rearrange("p k t -> p (k t)"), hT_ps[:, :], ACT.Copy).then_inc(aT_hi_done, 1)
            split_high(0, 0, 2)
            sc.wait_ge(y_done, TILES)
            ffn_h_high(0, o_ps)
            sc.wait_ge(gwT_copied, 1 + FC)

            def batch(b, more):
                bring_tables(ACT.Gelu)
                wait_apart(sc, gate_ready, b + 1, waited)
                chosen = [sc.value_load(top_idx[0:1, s:s + 1], min_val=0, max_val=NE - 1) for s in range(2)]
                gelu_of(b, 0, 0, chosen[0])
                split_high(b, 1, 0)
                split_high(b, 1, 1)
                gelu_of(b, 0, 1, chosen[0])
                split_high(b, 1, 2)
                for c in range(2, FC):
                    gelu_of(b, 0, c, chosen[0])
                if more:
                    ffn_h_high(b + 1, t_ps)
                    bring_tables(ACT.Exp)
                    exponents(b + 1)
                    bring_tables(ACT.Gelu)
                for c in range(FC):
                    gelu_of(b, 1, c, chosen[1])
                if more:
                    for piece in range(len(PARTS)):
                        split_high(b + 1, 0, piece)

            warm_before = warming.at
            WARMED_IN_BATCH = 3
            with sc.Fori(0, B - 1) as b:
                warming.at = warm_before + b * WARMED_IN_BATCH
                batch(b, True)
            warming.at = warm_before + (B - 1) * WARMED_IN_BATCH
            batch(B - 1, False)

        @block.tensor
        def _(pe):
            pe.wait_ge(consts_made, 4)
            pe.wait_ge(ones_made, 1)
            pe.wait_ge(gates_here, 32)
            pe.matmul(z_ps[:, 0:2], ones[0:1, :], gates_in[0:1, :], start=True, stop=True).then_inc(tanh_in, 1)
            pe.wait_ge(rowcnt_done, 1)
            pe.matmul(hT_ps[:, 0:E], below[:, :], rowcnt[:, :], start=True, stop=True)
            pe.matmul(hT_ps[:, E:2 * E], early[:, :], rowcnt[:, :], start=True, stop=True)
            pe.matmul(hT_ps[:, 2 * E:3 * E], ones[:, :], rowcnt[:, :], start=True, stop=True).then_inc(counts_done, 1)
            pe.wait_ge(gw_here, 32)
            for k in range(KD):
                last = pe.matmul(y_ps[:, k * NE:(k + 1) * NE], gw_rows[:, k * P:(k + 1) * P], ident[0:NE, 0:NE],
                                 start=True, stop=True)
            for c in range(FC):
                last = pe.matmul(y_ps[0:FM[c], (KD + c) * NE:(KD + c + 1) * NE], b1_rows[:, c * P:c * P + FM[c]],
                                 ident[0:NE, 0:NE], start=True, stop=True)
            last.then_inc(gwT_done, 1)
            def invert():
                pe.wait_ge(slot_hot_done, IDC)
                pe.wait_ge(tile_hot_done, 2)
                for c in range(IDC):
                    last = pe.matmul(aT_ps[:, 0:DIGITS * TILES], slot_hot[:, c, :],
                                     tile_hot[:, c].rearrange("p g j -> p (g j)"), start=(c == 0), stop=(c == IDC - 1))
                last.then_inc(rows_done, 1)

            def split_product(dst, stationary, moving, first, last):
                s_hi, s_lo = stationary
                m_hi, m_lo = moving
                pe.matmul(dst, s_hi, m_lo, start=first, stop=False)
                pe.matmul(dst, s_hi, m_hi, start=False, stop=False)
                return pe.matmul(dst, s_lo, m_hi, start=False, stop=last)

            def transpose_h(j):
                pe.wait_ge(h_ready, j + 1)
                at_least(pe, hT_lo_done, j)
                for k in range(KD):
                    last = pe.transpose(hT_ps[:, k * P:(k + 1) * P], h[:, k * P:(k + 1) * P], ident[:, :])
                last.then_inc(hT_done, 1)

            def transpose_a(j, bank=aT_ps):
                pe.wait_ge(a_ready, j + 1)
                at_least(pe, aT_lo_done, j)
                for k in range(KF1):
                    last = pe.transpose(bank[:, k * P:(k + 1) * P], a[:, k * P:(k + 1) * P], ident[:, :])
                last.then_inc(aT_done, 1)

            def expert_of(j):
                return pe.value_load(te_i[0:1, bass.ds(j, 1)], min_val=0, max_val=E - 1)

            def expert_product(e, dst, src_hi, src_lo, lo_done, count, first_wait=None, between=None):
                def product(k, src, weights, first, last):
                    return pe.matmul(dst[:, :], src[:, k, :], weights[:, bass.ds(e * (KD * F1) + k * F1, F1)],
                                     start=first, stop=last)

                for k in range(KD):
                    product(k, src_hi, ctx_hi, k == 0, False)
                if first_wait:
                    first_wait()
                for k in range(KD):
                    product(k, src_hi, ctx_lo, False, False)
                pe.wait_ge(lo_done, count)
                for k in range(KD):
                    if between and k == KD - 1:
                        between()
                    last = product(k, src_lo, ctx_hi, False, k == KD - 1)
                return last

            def first_product(j, e, first_wait=None):
                pe.wait_ge(hT_hi_done, j + 1)
                at_least(pe, a_ready, j)
                expert_product(e, z_ps, hT_hi, hT_lo, hT_lo_done, j + 1, first_wait).then_inc(z_done, 1)

            def second_product(j, e, between=None):
                pe.wait_ge(aT_hi_done, j + 1)
                at_least(pe, y_taken, j)
                expert_product(e, y_ps, aT_hi, aT_lo, aT_lo_done, j + 1, between=between).then_inc(y_done, 1)

            for n in range(E * KD):
                if n == 4:
                    invert()
                e, k = divmod(n, KD)
                if k == 0:
                    pe.wait_ge(ctx_here[e], 16)
                if 4 <= n < 4 + BY_ACT:
                    pe.wait_ge(ctx_lo_by_act, n - 3)
                elif n >= 4:
                    pe.wait_ge(ctx_lo_done, n - 3 - BY_ACT)
                for m in range(KF1):
                    last = pe.transpose(o_ps[n % 4][:, m * P:(m + 1) * P], raw_ctx[:, e, m, k * P:(k + 1) * P], ident[:, :])
                last.then_inc(ctxT_done, 1)
                if 1 <= n <= BY_ACT:
                    pe.wait_ge(ctx_hi_done, n)
                    e, k = divmod(n - 1, KD)
                    for m in range(KF1):
                        pe.matmul(o_ps[(n - 1) % 4][:, m * P:(m + 1) * P], raw_ctx[:, e, m, k * P:(k + 1) * P],
                                  ident[:, :], is_transpose=True, start=(m == 0), stop=False)
                    pe.matmul(o_ps[(n - 1) % 4][:, :], neg_ident[:, :], ctx_hi[:, (n - 1) * F1:n * F1],
                              start=False, stop=True).then_inc(ctx_rest_done, 1)

            transpose_h(0)
            pe.wait_ge(routed, 2)
            e = expert_of(0)
            pe.wait_ge(ctx_hi_done, E * KD)

            def low_context():
                pe.wait_ge(ctx_lo_by_act, BY_ACT)
                pe.wait_ge(ctx_lo_done, E * KD - BY_ACT)

            first_product(0, e, low_context)
            transpose_h(1)
            with pe.Fori(1, PREP) as j:
                e_before, e = expert_of(j - 1), expert_of(j)
                transpose_a(j - 1)
                first_product(j, e)
                transpose_h(j + 1)
                second_product(j - 1, e_before)

            def transpose_h2(b, ks):
                pe.wait_ge(h2_ready, TT * b + TT)
                for k in ks:
                    if k == 1:
                        pe.wait_ge(mix_ready, b)
                    pe.wait_ge(h2T_lo_done, KD * b + max(k - 1, 0))
                    for t in range(TT):
                        last = pe.transpose(t_ps[k % 2][:, t * P:(t + 1) * P],
                                            h2[:, t * D + k * P:t * D + (k + 1) * P], ident[:, :])
                    last.then_inc(h2T_done, 1)

            def transpose_first_h2():
                pe.wait_ge(h2_ready, TT)
                for k in range(KD):
                    for t in range(TT):
                        last = pe.transpose(o_ps[k][:, t * P:(t + 1) * P],
                                            h2[:, t * D + k * P:t * D + (k + 1) * P], ident[:, :])
                    last.then_inc(h2T_done, 1)

            def logits(b):
                if isinstance(b, int) and b == 0:
                    pe.wait_ge(sums_done, KD)
                    pe.wait_ge(hT_lo_done, PREP + 4)
                else:
                    pe.wait_ge(h2T_hi_done, KD * b + KD)
                    pe.wait_ge(h2T_lo_done, KD * b + KD - 1)
                for k in range(KD):
                    last = pe.matmul(t_ps[0][0:1, 0:NE], hsum[:, k:k + 1], gwT[:, k, :], start=(k == 0), stop=(k == KD - 1))
                last.then_inc(logit_done, 1)

            def spread_mix(b):
                pe.wait_ge(mix1_ready, b + 1)
                pe.matmul(t_ps[1][:, 0:2], ones[0:1, :], mix1[:, :], start=True, stop=True).then_inc(mix_spread, 1)

            def hidden(b, s, between=None):
                for c in range(FC):
                    k6 = s * FC + c
                    wait_primed(pe, gelu_done, 2 * FC * b + max(k6 - 1, 0))
                    if c < 2:
                        pe.wait_ge(lo_done[s], len(PARTS) * b + c + 1)
                    for k in range(KD):
                        if c == 0:
                            pe.wait_ge(h2T_lo_done, KD * b + k + 1)
                        col0 = k * P if c == 0 else KD * P + k * (F2 - P) + (c - 1) * P
                        rows = bass.ds((b % 2) * (KD * S) + k * S, S)
                        last = split_product(hid_ps[k6 % 2][0:FM[c], :],
                                             (w_hi[s][:, col0:col0 + FM[c]], w_lo[s][:, col0:col0 + FM[c]]),
                                             (h2T_hi[:, rows], h2T_lo[:, rows]), k == 0, k == KD - 1)
                    last.then_inc(hid_done, 1)
                    if between and c == 0:
                        between(b + 1)

            def output(b, s, cs, ts=range(TT)):
                pe.wait_ge(lo_done[s], len(PARTS) * (b + 1))
                for c in cs:
                    pe.wait_ge(a2_ready, (2 * b + s) * FC + c + 2)
                if s == 0 and cs[0] == 0:
                    wait_primed(pe, o_taken, TT * b)
                for t in ts:
                    for c in cs:
                        rows = P if c < FC - 1 else BIAS_ROW + 1
                        place = slice(W1N + c * D, W1N + (c + 1) * D)
                        last = split_product(o_ps[t][:, :],
                                             (a2_hi[0:rows, c, t * P:(t + 1) * P], a2_lo[0:rows, c, t * P:(t + 1) * P]),
                                             (w_hi[s][0:rows, place], w_lo[s][0:rows, place]),
                                             s == 0 and c == 0, s == 1 and c == FC - 1)
                    if s == 1 and cs[-1] == FC - 1:
                        last.then_inc(o_done, 1)
                return last

            e_before, e = expert_of(PREP - 1), expert_of(PREP)
            for j in range(PREP, TILES):
                if j == PREP + 5:
                    pe.wait_ge(mix_ready, 1)
                transpose_a(j - 1)
                first_product(j, e)
                if j == PREP + 3:
                    pe.wait_ge(neg_max_ready, 1)
                if j + 1 < TILES:
                    transpose_h(j + 1)
                    second_product(j - 1, e_before)
                    e_before, e = e, expert_of(j + 1)
                else:
                    second_product(j - 1, e_before, lambda: transpose_a(TILES - 1, hT_ps))
                if j == PREP + 1:
                    transpose_first_h2()
                if j == PREP + 2:
                    logits(0)
                if j == PREP + 4:
                    pe.wait_ge(aT_lo_done, PREP + 4)
                    spread_mix(0)
            pe.wait_ge(aT_hi_done, TILES)
            expert_product(e, aT_ps, hT_hi, hT_lo, aT_lo_done, TILES).then_inc(y_done, 1)
            pe.wait_ge(y_taken, TILES - 1)
            full = list(range(FC - 1))

            def batch(b, more):
                hidden(b, 0)
                output(b, 0, full)
                if more:
                    transpose_h2(b + 1, (0, 1))
                output(b, 0, [FC - 1], range(0, TT // 2))
                if more:
                    transpose_h2(b + 1, (2, 3))
                output(b, 0, [FC - 1], range(TT // 2, TT)).then_inc(pair_done, 1)
                if more:
                    logits(b + 1)
                hidden(b, 1, spread_mix if more else None)
                output(b, 1, full)
                output(b, 1, [FC - 1])
                pe.drain().then_inc(pair_done, 1)

            with pe.Fori(0, B - 1) as b:
                batch(b, True)
            batch(B - 1, False)


_INS = ["x", "itok_BxS_13_99985", "ctx_2048", "g_xattn", "g_ffn", "L0_ffn_gate_W", "L0_ffn_W1", "L0_ffn_b1",
        "L0_ffn_W2", "L0_ffn_b2"]


def kernel(**inputs):
    import numpy as _np
    import concourse.bacc as _bacc
    from concourse import mybir as _mybir
    from concourse.bass_utils import run_bass_kernel_spmd as _run

    nc = _bacc.Bacc("TRN2", target_bir_lowering=False, num_devices=1)
    arrays, args = {}, []
    for name in _INS:
        a = _np.ascontiguousarray(inputs[name])
        arrays[f"in_{name}"] = a
        args.append(nc.dram_tensor(f"in_{name}", a.shape, _mybir.dt.from_np(a.dtype), kind="ExternalInput").ap())
    shape = inputs["x"].shape
    args.append(nc.dram_tensor("out_0", shape, _mybir.dt.float32, kind="ExternalOutput").ap())
    flamingo_kernel(nc, *args)
    r = _run(nc, [arrays], core_ids=[0])
    return r.results[0]["out_0"]
```

```python
from contextlib import ExitStack

import concourse.bass as bass
from concourse import mybir

FP32 = mybir.dt.float32
FP32R = mybir.dt.float32r
BF16 = mybir.dt.bfloat16
FP16 = mybir.dt.float16
I32 = mybir.dt.int32
U32 = mybir.dt.uint32
ALU = mybir.AluOpType
ACT = mybir.ActivationFunctionType
AX_X = mybir.AxisListType.X

P = 128
EPS = 1e-5
VOCAB = 25000


def at_least(engine, sem, value):
    if not (isinstance(value, int) and value <= 0):
        engine.wait_ge(sem, value)


def wait_apart(engine, sem, value, counted):
    engine.wait_ge(sem, value)
    if not isinstance(value, int):
        engine.sem_inc(counted, 1)


class Chain:

    def __init__(self, engine, sem, counted):
        self.engine, self.sem, self.counted, self.at = engine, sem, counted, 0

    def sign(self, ins):
        self.at = self.at + 1
        ins.then_inc(self.sem, 1)
        return self.at

    def wait(self, count, apart=False):
        if apart:
            wait_apart(self.engine, self.sem, count, self.counted)
        else:
            self.engine.wait_ge(self.sem, count)

    def run(self, ins, apart=False):
        self.wait(self.sign(ins), apart)


def flamingo_kernel(nc, x, ids, ctx, g_xattn, g_ffn, gate_w, w1, b1, w2, b2, out):
    B, S, D = x.shape
    E = ctx.shape[0]
    F1 = ctx.shape[1]
    NE, _, F2 = w1.shape
    N = B * S
    KD = D // P
    DS = D + 2
    KF1 = F1 // P
    IDC = N // P
    IDC_BY_POOL = IDC // 4
    TILES = N // P + E - 1
    RING = 6
    LOOPED = (TILES - RING + 1) // RING * RING
    AHEAD = 4
    TT = S // P
    EARLY = TT + E - 1
    PREP = TILES - 7
    BY_ACT = 2
    FC = -(-F2 // P)
    FM = [min(P, F2 - c * P) for c in range(FC)]
    BIAS_ROW = FM[-1]
    W1N = KD * F2
    WN = W1N + FC * D
    PARTS = [slice(0, KD * P), slice(KD * P, W1N), slice(W1N, WN)]
    EXPERT_IDS = VOCAB // E
    assert N <= 2048
    assert EARLY < RING + 2 and TILES - 7 > EARLY + 2 and F1 == D and BIAS_ROW % 32 == 0 and FM[-1] < P and B >= 2

    x_rows = x.rearrange("b s d -> (b s) d")
    x1_rows = nc.dram_tensor("x1_scratch", [N + TILES * P, DS], FP32, kind="Internal").ap()

    with ExitStack() as stack:
        def sb(name, shape, dt=FP32):
            return stack.enter_context(nc.sbuf_tensor(name, shape, dt))

        def sem(name):
            return stack.enter_context(nc.semaphore(name))

        banks = [stack.enter_context(nc.psum_tensor(f"bank{i}", [P, 512], FP32)) for i in range(8)]
        hT_ps, aT_ps, z_ps, y_ps = banks[0:4]
        t_ps, hid_ps, o_ps = banks[0:2], banks[2:4], banks[4:8]

        ctx_hi = sb("ctx_hi", [P, E * KD * F1], FP32R)
        ctx_lo = sb("ctx_lo", [P, E * KD * F1], FP32R)
        raw_ctx = sb("raw_ctx", [P, E, KF1, D])
        arena = raw_ctx[:, :, :, :].rearrange("p e k d -> p (e k d)")
        X1B = TT * DS
        x1b = arena[:, 0:2 * X1B]
        h2 = arena[:, 2 * X1B:2 * X1B + TT * D]
        act = arena[:, 2 * X1B + TT * D:2 * X1B + TT * D + 2 * S].rearrange("p (c t) -> p c t", t=S)
        h2T_hi = ctx_hi[:, 0:2 * KD * S]
        h2T_lo = ctx_lo[:, 0:2 * KD * S]

        w_raw = [sb(f"w_raw{s}", [P, WN]) for s in range(2)]
        w_hi = [sb(f"w_hi{s}", [P, WN], FP32R) for s in range(2)]
        w_lo = [sb(f"w_lo{s}", [P, WN], FP32R) for s in range(2)]
        b1_rows = sb("b1_rows", [NE, F2])
        b1T = sb("b1T", [P, FC, NE])
        act_last = sb("act_last", [P, S])
        a2_hi = ctx_hi[:, 2 * KD * S:(2 * KD + FC) * S].rearrange("p (c t) -> p c t", t=S)
        a2_lo = ctx_lo[:, 2 * KD * S:(2 * KD + FC) * S].rearrange("p (c t) -> p c t", t=S)

        x_ring = sb("x_ring", [P, RING * DS])
        h = sb("h", [P, D])
        hT_hi = sb("hT_hi", [P, KD, P], FP32R)
        hT_lo = sb("hT_lo", [P, KD, P], FP32R)
        a = sb("a", [P, F1])
        aT_hi = sb("aT_hi", [P, KF1, P], FP32R)
        aT_lo = sb("aT_lo", [P, KF1, P], FP32R)

        col_i = sb("col_i", [P, P], I32)
        col = sb("col", [P, P])
        part_i = sb("part_i", [P, 1], I32)
        part = sb("part", [P, 1])
        ident = sb("ident", [P, P])
        neg_ident = sb("neg_ident", [P, P], FP32R)
        below = sb("below", [P, P], BF16)
        early = sb("early", [P, P], BF16)
        ones_h = sb("ones_h", [P, P], BF16)
        ones = sb("ones", [P, P])
        half = sb("half", [P, 1])
        slot_i = sb("slot_i", [P, TILES], I32)
        slot = sb("slot", [P, TILES])
        ids_i = sb("ids_i", [P, IDC], I32)
        ids_f = sb("ids_f", [P, IDC])
        least = sb("least", [P, E + 1, IDC])
        member = sb("member", [P, E, IDC])
        scan0 = sb("scan0", [P, 1 + E * IDC])
        scan = scan0[:, 1:1 + E * IDC].rearrange("p (e c) -> p e c", c=IDC)
        rowcnt = sb("rowcnt", [P, E], BF16)
        cnt_i = sb("cnt_i", [P, 2 * E], I32)
        ntile_i = sb("ntile_i", [P, 2 * E], I32)
        ntile = sb("ntile", [P, 2 * E])
        ends = sb("ends", [P, 2 * E])
        starts = sb("starts", [P, 2 * E])
        shift = sb("shift", [P, E])
        base = sb("base", [P, E])
        ranks = sb("ranks", [P, E, IDC])
        rank = sb("rank", [P, IDC])
        rank_i = sb("rank_i", [P, IDC], I32)
        pslot_i = sb("pslot_i", [P, IDC], I32)
        ptile_i = sb("ptile_i", [P, IDC], I32)
        pslot = sb("pslot", [P, IDC])
        own_tile = sb("own_tile", [P, IDC])
        jump = sb("jump", [P, E, IDC])
        ahead = sb("ahead", [P, IDC])
        ptile = sb("ptile", [P, IDC])
        DIGITS = 2
        tile_hot = w_raw[0][:, 0:IDC * DIGITS * TILES // 2].bitcast(FP16).rearrange("p (c g j) -> p c g j", g=DIGITS, j=TILES)
        slot_hot = w_raw[1][:, 0:IDC * P // 2].bitcast(FP16).rearrange("p (c s) -> p c s", s=P)
        token_i = sb("token_i", [P, IDC], I32)
        token_h = sb("token_h", [P, IDC], FP16)
        col_h = sb("col_h", [P, P], FP16)
        unused = sb("unused", [P, TILES])
        ended = sb("ended", [P, TILES, 2 * E])
        te = sb("te", [P, TILES])
        te_i = sb("te_i", [P, TILES], I32)
        rows_f = sb("rows_f", [P, TILES])
        put_rows = sb("put_rows", [P, TILES], U32)
        get_rows = sb("get_rows", [P, TILES], U32)
        put_idx = sb("put_idx", [P, RING], U32)
        get_idx = sb("get_idx", [P, RING], U32)
        gates_in = sb("gates_in", [1, 2])
        tg = sb("tg", [P, 2])

        stats1 = sb("stats1", [P, 6])
        mv1 = sb("mv1", [P, 2])
        ve1 = sb("ve1", [P, 1])
        rstd1 = sb("rstd1", [P, 1])
        stats2 = sb("stats2", [P, 6])
        mv2 = sb("mv2", [P, 2])
        eps_row = sb("eps_row", [P, 2])
        warm = sb("warm", [1, 2])
        gw_rows = sb("gw_rows", [NE, D])
        gwT = sb("gwT", [P, KD, NE])
        hsum = sb("hsum", [P, KD])
        logit = sb("logit", [1, NE])
        neg_max = sb("neg_max", [1, 1])
        expo = sb("expo", [1, NE])
        esum = sb("esum", [1, 1])
        einv = sb("einv", [1, 1])
        prob = sb("prob", [1, 8])
        top = sb("top", [1, 8])
        top_idx = sb("top_idx", [1, 8], U32)
        tsum = sb("tsum", [1, 1])
        tinv = sb("tinv", [1, 1])
        mix1 = sb("mix1", [1, 2])
        mix = sb("mix", [P, 2 * 2])

        ids_here, gates_here, gw_here = sem("ids_here"), sem("gates_here"), sem("gw_here")
        ctx_here = [sem(f"ctx_here{e}") for e in range(E)]
        iota_made, ones_made, consts_made = sem("iota_made"), sem("ones_made"), sem("consts_made")
        tables_made = sem("tables_made")
        dve_step, pool_step = sem("dve_step"), sem("pool_step")
        ctxT_done, ctx_hi_done, ctx_lo_done = sem("ctxT_done"), sem("ctx_hi_done"), sem("ctx_lo_done")
        rowcnt_done, counts_done, tile_hot_done = sem("rowcnt_done"), sem("counts_done"), sem("tile_hot_done")
        pslot_done, token_made = sem("pslot_done"), sem("token_made")
        slot_hot_done, rows_done = sem("slot_hot_done"), sem("rows_done")
        routed, tanh_in, tg_done = sem("routed"), sem("tanh_in"), sem("tg_done")
        gwT_done, gwT_copied = sem("gwT_done"), sem("gwT_copied")
        gathered = [sem(f"gathered{r}") for r in range(RING)]
        scattered = [sem(f"scattered{r}") for r in range(RING)]
        x_ready, ve_ready, rstd_ready = sem("x_ready"), sem("ve_ready"), sem("rstd_ready")
        h_ready, hT_done, hT_hi_done, hT_lo_done = sem("h_ready"), sem("hT_done"), sem("hT_hi_done"), sem("hT_lo_done")
        z_done, silu_done, a_ready = sem("z_done"), sem("silu_done"), sem("a_ready")
        aT_done, aT_hi_done, aT_lo_done = sem("aT_done"), sem("aT_hi_done"), sem("aT_lo_done")
        y_done, y_taken, x1_ready = sem("y_done"), sem("y_taken"), sem("x1_ready")
        x1_here, h2_ready = [sem(f"x1_here{t}") for t in range(TT)], sem("h2_ready")
        h2T_done, h2T_hi_done, h2T_lo_done = sem("h2T_done"), sem("h2T_hi_done"), sem("h2T_lo_done")
        logit_done, neg_max_ready = sem("logit_done"), sem("neg_max_ready")
        expo_done, gate_ready, mix1_ready = sem("expo_done"), sem("gate_ready"), sem("mix1_ready")
        mix_spread, mix_ready = sem("mix_spread"), sem("mix_ready")
        w1_here = [sem(f"w1_here{s}") for s in range(2)]
        w1_rest_here = [sem(f"w1_rest_here{s}") for s in range(2)]
        w2_here = [sem(f"w2_here{s}") for s in range(2)]
        hi_done = [sem(f"hi_done{s}") for s in range(2)]
        lo_done = [sem(f"lo_done{s}") for s in range(2)]
        hid_done, gelu_done, a2_ready = sem("hid_done"), sem("gelu_done"), sem("a2_ready")
        pair_done, o_done, o_taken, out_stored = sem("pair_done"), sem("o_done"), sem("o_taken"), sem("out_stored")
        pads_made, waited = sem("pads_made"), sem("waited")
        tiles_landed, warmed, sums_done = sem("tiles_landed"), sem("warmed"), sem("sums_done")
        ctx_rest_done, ctx_lo_by_act = sem("ctx_rest_done"), sem("ctx_lo_by_act")

        block = stack.enter_context(nc.Block())
        W2_DMAS = 3

        primed = (pair_done, o_taken, out_stored, gelu_done, a2_ready)

        def wait_primed(engine, sem, value):
            engine.wait_ge(sem, value + 1)

        @block.sync
        def _(sp):
            sp.dma_start(ids_i[:, :], ids.rearrange("b s -> (b s)").rearrange("(p c) -> p c", c=IDC)).then_inc(ids_here, 16)
            for e in range(E):
                sp.dma_start(raw_ctx[:, e], ctx[e].rearrange("(k p) d -> p k d", p=P)).then_inc(ctx_here[e], 16)

            for counted in primed:
                sp.sem_inc(counted, 1)

            def announce(k, r):
                sp.wait_ge(gathered[r], 16 * k + 16)
                sp.sem_inc(x_ready, 1)

            with sp.Fori(0, PREP // RING) as k:
                for r in range(RING):
                    announce(k, r)

            def load_x1(b):
                for t in range(TT):
                    sp.dma_start(x1b[:, bass.ds((b % 2) * X1B + t * DS, DS)],
                                 x1_rows[bass.ds(b * S + t * P, P), :]).then_inc(x1_here[t], 16)

            def load_experts(b):
                wait_apart(sp, gate_ready, b + 1, waited)
                full = (FC - 1) * P
                chosen = [sp.value_load(top_idx[0:1, s:s + 1], min_val=0, max_val=NE - 1) for s in range(2)]
                for s, e in enumerate(chosen):
                    if not isinstance(b, int):
                        wait_apart(sp, lo_done[s], len(PARTS) * b, waited)
                    raw = w_raw[s]
                    for place, width, here in ((PARTS[0], slice(0, P), w1_here[s]), (PARTS[1], slice(P, F2), w1_rest_here[s])):
                        sp.dma_start(raw[:, place].rearrange("p (k f) -> p k f", k=KD),
                                     w1[bass.ds(e, 1), :, width].rearrange("o (k p) f -> p (o k) f", p=P)).then_inc(here, 16)
                    sp.dma_start(raw[:, W1N:W1N + (FC - 1) * D].rearrange("p (c d) -> p c d", d=D),
                                 w2[bass.ds(e, 1), 0:full].rearrange("o (c p) d -> p (o c) d", p=P)).then_inc(w2_here[s], 16)
                    last = raw[:, W1N + (FC - 1) * D:WN]
                    sp.dma_start(last[0:FM[-1], :], w2[bass.ds(e, 1), full:F2].rearrange("o f d -> (o f) d")).then_inc(w2_here[s], 16)
                    sp.dma_start(last[BIAS_ROW:BIAS_ROW + 1, :], b2[bass.ds(e, 1), :]).then_inc(w2_here[s], 16)

            def store(b):
                for t in range(TT):
                    wait_apart(sp, o_taken, TT * b + t + 2, waited)
                    sp.dma_start(out.rearrange("b s d -> (b s) d")[bass.ds(b * S + t * P, P), :],
                                 x1b[:, bass.ds((b % 2) * X1B + t * DS, D)]).then_inc(out_stored, 16)

            sp.wait_ge(ctxT_done, E * KD)
            sp.wait_ge(tiles_landed, EARLY)
            load_x1(0)
            for j in range(PREP // RING * RING, TILES):
                announce(j // RING, j % RING)
            sp.wait_ge(rows_done, 1)
            sp.wait_ge(pads_made, 3)
            load_experts(0)
            sp.wait_ge(tiles_landed, TILES)
            with sp.Fori(0, B - 1) as b:
                wait_apart(sp, h2_ready, TT * b + TT, waited)
                wait_apart(sp, out_stored, 16 * TT * b + 1, waited)
                load_x1(b + 1)
                load_experts(b + 1)
                store(b)
            store(B - 1)
            wait_primed(sp, out_stored, 16 * TT * B)

        @block.gpsimd
        def _(pool):
            pool.iota(col_i[:, :], [[1, P]], base=0, channel_multiplier=0).then_inc(iota_made, 1)
            pool.iota(part_i[:, :], [[0, 1]], base=0, channel_multiplier=1).then_inc(iota_made, 1)
            pool.iota(slot_i[:, :], [[P, TILES]], base=N, channel_multiplier=1).then_inc(iota_made, 1)
            pool.memset(ones[:, :], 1.0).then_inc(ones_made, 1)
            pool.memset(ones_h[:, :], 1.0).then_inc(ones_made, 1)
            pool.iota(token_i[:, :], [[1, IDC]], base=0, channel_multiplier=IDC).then_inc(token_made, 1)
            pool.memset(half[:, :], -0.5).then_inc(pool_step, 1)
            pool.wait_ge(pool_step, 1)
            chain = Chain(pool, pool_step, waited)
            chain.at = 1

            for s in range(2):
                pool.memset(w_raw[s][BIAS_ROW:P, W1N + (FC - 1) * D:WN], 0.0).then_inc(pads_made, 1)
            pool.wait_ge(pads_made, 3)
            pool.wait_ge(pslot_done, 1)
            for c in range(IDC_BY_POOL):
                pool.tensor_scalar(slot_hot[:, c, :], col_h[:, :], pslot[:, c:c + 1], None, ALU.is_equal).then_inc(slot_hot_done, 1)

            def gather(j, r):
                if isinstance(j, int):
                    rows = get_rows[:, j:j + 1]
                else:
                    chain.run(pool.tensor_copy(get_idx[:, r:r + 1], get_rows[:, bass.ds(j, 1)]), apart=True)
                    rows = get_idx[:, r:r + 1]
                pool.indirect_dma_start(x_ring[:, r * DS:r * DS + D], None, x_rows,
                                        bass.IndirectOffsetOnAxis(rows, 0)).then_inc(gathered[r], 16)

            def inverse_root(j):
                pool.wait_ge(ve_ready, j + 1)
                pool.tensor_tensor(rstd1[:, :], ve1[:, :], half[:, 0:1],
                                   ALU.pow).then_inc(rstd_ready, 1)

            def scatter(j, r):
                chain.run(pool.tensor_copy(put_idx[:, r:r + 1], put_rows[:, bass.ds(j, 1)]))
                pool.wait_ge(x1_ready, j + 1)
                deviation = x_ring[:, (r + 1) * DS - 1:(r + 1) * DS]
                chain.run(pool.tensor_tensor(deviation, deviation, half[:, 0:1], ALU.pow), apart=True)
                pool.indirect_dma_start(x1_rows, bass.IndirectOffsetOnAxis(put_idx[:, r:r + 1], 0),
                                        x_ring[:, r * DS:(r + 1) * DS], None).then_inc(scattered[r], 16)

            def landed(j):
                pool.wait_ge(scattered[j % RING], 16 * (j // RING) + 16)
                pool.sem_inc(tiles_landed, 1)

            pool.wait_ge(routed, 2)
            for j in range(RING - 1):
                gather(j, j)
                if j >= 2:
                    inverse_root(j - 2)
            inverse_root(RING - 3)
            scatter(0, 0)
            inverse_root(AHEAD)
            gather(RING - 1, RING - 1)
            STEPS = 3
            steps = chain.at
            with pool.Fori(0, LOOPED // RING) as k:
                chain.at = steps + k * (STEPS * RING)
                for r in range(1, RING + 1):
                    j = k * RING + r
                    scatter(j, r % RING)
                    inverse_root(j + AHEAD)
                    pool.wait_ge(scattered[r - 1], 16 * k + 16)
                    pool.sem_inc(tiles_landed, 1)
                    gather(j + RING - 1, r - 1)
            chain.at = steps + LOOPED // RING * (STEPS * RING)
            for j in range(LOOPED + 1, TILES):
                scatter(j, j % RING)
                landed(j - 1)
                if j + RING - 1 < TILES:
                    gather(j + RING - 1, (j - 1) % RING)
                if j + AHEAD < TILES:
                    inverse_root(j + AHEAD)
            landed(TILES - 1)

        @block.vector
        def _(dve):
            chain = Chain(dve, dve_step, waited)
            run = chain.run
            dve.wait_ge(iota_made, 3)
            dve.tensor_copy(part[:, :], part_i[:, :]).then_inc(dve_step, 1)
            chain.at = 1
            run(dve.tensor_copy(col[:, :], col_i[:, :]))
            dve.tensor_scalar(ident[:, :], col[:, :], part[:, 0:1], None, ALU.is_equal).then_inc(consts_made, 1)
            dve.tensor_scalar(below[:, :], col[:, :], part[:, 0:1], None, ALU.is_gt).then_inc(consts_made, 1)
            dve.tensor_scalar(neg_ident[:, :], col[:, :], part[:, 0:1], -1.0, ALU.is_equal, ALU.mult).then_inc(consts_made, 1)
            dve.wait_ge(ones_made, 2)
            dve.tensor_scalar(early[:, :], ones[:, :], part[:, 0:1], float(S // IDC), ALU.mult, ALU.is_lt).then_inc(consts_made, 1)
            dve.tensor_copy(col_h[:, :], col[:, :]).then_inc(tables_made, 1)
            dve.memset(eps_row[:, 0:1], 0.0).then_inc(tables_made, 1)
            dve.memset(eps_row[:, 1:2], EPS).then_inc(tables_made, 1)
            dve.tensor_copy(slot[:, :], slot_i[:, :]).then_inc(tables_made, 1)
            dve.memset(least[:, 0, :], 1.0).then_inc(tables_made, 1)
            dve.memset(least[:, E, :], 0.0).then_inc(tables_made, 1)
            dve.memset(scan0[:, 0:1], 0.0).then_inc(tables_made, 1)
            dve.wait_ge(token_made, 1)
            dve.tensor_copy(token_h[:, :], token_i[:, :]).then_inc(tables_made, 1)

            dve.wait_ge(ids_here, 16)
            run(dve.tensor_copy(ids_f[:, :], ids_i[:, :]))
            for e in range(1, E):
                dve.tensor_scalar(least[:, e, :], ids_f[:, :], float(e * EXPERT_IDS), None, ALU.is_ge).then_inc(tables_made, 1)
            dve.wait_ge(tables_made, 8 + E - 1)
            run(dve.tensor_tensor(member[:, :, :], least[:, 0:E, :], least[:, 1:E + 1, :], ALU.subtract))
            with nc.allow_low_precision(reason="counts up to the number of columns are exact in bfloat16"):
                dve.tensor_reduce(rowcnt[:, :], member[:, :, :], AX_X, ALU.add).then_inc(rowcnt_done, 1)
            flat = member[:, :, :].rearrange("p e c -> p (e c)")
            run(dve.tensor_tensor_scan(scan0[:, 1:1 + E * IDC], ones[:, 0:E * IDC], flat, 0.0, ALU.mult, ALU.add))
            dve.memset(prob[:, :], -1.0).then_inc(pads_made, 1)
            dve.wait_ge(counts_done, 1)
            prefix, counts = hT_ps[:, 0:E], hT_ps[:, E:3 * E]
            SHIFT = P.bit_length() - 1

            def by_expert(values):
                return values.unsqueeze(2).to_broadcast([P, E, IDC])

            tiles = chain.sign(dve.tensor_scalar(cnt_i[:, :], counts, float(P - 1), None, ALU.add))
            ranked = chain.sign(dve.scalar_tensor_tensor(base[:, :], prefix, -1.0, scan0[:, 0:E * IDC:IDC], ALU.add, ALU.subtract))
            chain.wait(tiles)
            tiles = chain.sign(dve.tensor_single_scalar(ntile_i[:, :], cnt_i[:, :], SHIFT, ALU.logical_shift_right))
            chain.wait(ranked)
            ranked = chain.sign(dve.tensor_tensor(ranks[:, :, :], scan[:, :, :], by_expert(base[:, :]), ALU.add))
            chain.wait(tiles)
            tiles = chain.sign(dve.tensor_copy(ntile[:, :], ntile_i[:, :]))
            chain.wait(ranked)
            ranked = chain.sign(dve.tensor_tensor(ranks[:, :, :], ranks[:, :, :], member[:, :, :], ALU.mult))
            chain.wait(tiles)
            tiles = chain.sign(dve.tensor_tensor(ntile[:, E:2 * E], ntile[:, E:2 * E], ntile[:, 0:E], ALU.subtract))
            chain.wait(ranked)
            ranked = chain.sign(dve.tensor_reduce(rank[:, :], ranks[:, :, :].rearrange("p e c -> p c e"), AX_X, ALU.add))
            chain.wait(tiles)
            tiles = chain.sign(dve.tensor_tensor_scan(ends[:, :], ones[:, 0:2 * E], ntile[:, :], 0.0, ALU.mult, ALU.add))
            chain.wait(ranked)
            ranked = chain.sign(dve.tensor_copy(rank_i[:, :], rank[:, :]))
            chain.wait(tiles)
            tiles = chain.sign(dve.tensor_tensor(starts[:, :], ends[:, :], ntile[:, :], ALU.subtract))
            chain.wait(ranked)
            ranked = chain.sign(dve.tensor_single_scalar(ptile_i[:, :], rank_i[:, :], SHIFT, ALU.logical_shift_right))
            slots = chain.sign(dve.tensor_single_scalar(pslot_i[:, :], rank_i[:, :], P - 1, ALU.bitwise_and))
            chain.wait(tiles)
            tiles = chain.sign(dve.tensor_tensor(shift[:, :], starts[:, E:2 * E], ends[:, 0:E], ALU.subtract))
            chain.wait(ranked)
            ranked = chain.sign(dve.tensor_copy(own_tile[:, :], ptile_i[:, :]))
            chain.wait(slots)
            dve.tensor_copy(pslot[:, :], pslot_i[:, :]).then_inc(pslot_done, 1)

            def slot_rows(c):
                dve.tensor_scalar(slot_hot[:, c, :], col_h[:, :], pslot[:, c:c + 1], None, ALU.is_equal).then_inc(slot_hot_done, 1)

            left = list(range(IDC_BY_POOL, IDC))
            own = own_tile[:, :].unsqueeze(1).to_broadcast([P, E, IDC])
            chain.wait(ranked)
            tiled = chain.sign(dve.tensor_tensor(jump[:, :, :], own, by_expert(ntile[:, 0:E]), ALU.is_ge))
            dve.wait_ge(pslot_done, 1)
            slot_rows(left.pop())
            chain.wait(tiled)
            tiled = chain.sign(dve.tensor_tensor(jump[:, :, :], jump[:, :, :], by_expert(shift[:, :]), ALU.mult))
            slot_rows(left.pop())
            chain.wait(tiled)
            tiled = chain.sign(dve.tensor_tensor(jump[:, :, :], jump[:, :, :], by_expert(starts[:, 0:E]), ALU.add))
            slot_rows(left.pop())
            chain.wait(tiled)
            tiled = chain.sign(dve.tensor_tensor(jump[:, :, :], jump[:, :, :], member[:, :, :], ALU.mult))
            slot_rows(left.pop())
            chain.wait(tiled)
            tiled = chain.sign(dve.tensor_reduce(ahead[:, :], jump[:, :, :].rearrange("p e c -> p c e"), AX_X, ALU.add))
            slot_rows(left.pop())
            chain.wait(tiled)
            tiled = chain.sign(dve.tensor_tensor(ptile[:, :], own_tile[:, :], ahead[:, :], ALU.add))
            slot_rows(left.pop())
            chain.wait(tiled)
            ones_part = tile_hot[:, :, 1, :]
            tiled = chain.sign(dve.tensor_tensor(ones_part, col_h[:, 0:TILES].unsqueeze(1).to_broadcast([P, IDC, TILES]),
                                                 ptile[:, :].unsqueeze(2).to_broadcast([P, IDC, TILES]), ALU.is_equal))
            slot_rows(left.pop())
            chain.wait(tiled)
            dve.tensor_tensor(tile_hot[:, :, 0, :], ones_part, token_h[:, :].unsqueeze(2).to_broadcast([P, IDC, TILES]),
                              ALU.mult).then_inc(tile_hot_done, 1)
            for c in left:
                slot_rows(c)
            run(dve.tensor_tensor(ended[:, :, :], col[:, 0:TILES].unsqueeze(2).to_broadcast([P, TILES, 2 * E]),
                                  ends[:, :].unsqueeze(1).to_broadcast([P, TILES, 2 * E]), ALU.is_ge))
            run(dve.tensor_reduce(te[:, :], ended[:, :, 0:2 * E - 1], AX_X, ALU.add))
            run(dve.scalar_tensor_tensor(te_i[:, :], ended[:, :, E - 1], -float(E), te[:, :], ALU.mult, ALU.add))
            dve.wait_ge(rows_done, 1)
            run(dve.scalar_tensor_tensor(unused[:, :], aT_ps[:, TILES:2 * TILES], 1.0, slot[:, :], ALU.subtract, ALU.mult))
            run(dve.tensor_tensor(rows_f[:, :], aT_ps[:, 0:TILES], unused[:, :], ALU.subtract))
            dve.tensor_scalar(get_rows[:, :], rows_f[:, :], float(N - 1), None, ALU.min).then_inc(routed, 1)
            dve.tensor_copy(put_rows[:, :], rows_f[:, :]).then_inc(routed, 1)
            def ring_row(j, start, size):
                return x_ring[:, bass.ds((j % RING) * DS + start, size)]

            def rows_statistics(j):
                wait_apart(dve, x_ready, j + 1, waited)
                run(dve.bn_stats(stats1[:, :], ring_row(j, 0, D)), apart=True)
                run(dve.bn_aggr(mv1[:, :], stats1[:, :]))
                dve.tensor_scalar(ve1[:, :], mv1[:, 1:2], EPS, None, ALU.add).then_inc(ve_ready, 1)

            def residual(j, bank=y_ps):
                dve.wait_ge(y_done, j + 1)
                place = ring_row(j, 0, D)
                dve.scalar_tensor_tensor(place, bank[:, :], tg[:, 0:1], place, ALU.mult, ALU.add).then_inc(y_taken, 1)
                wait_apart(dve, y_taken, j + 1, waited)
                run(dve.bn_stats(stats2[:, :], ring_row(j, 0, D)), apart=True)
                run(dve.bn_aggr(mv2[:, :], stats2[:, :]))
                dve.tensor_tensor(ring_row(j, D, 2), mv2[:, :], eps_row[:, :], ALU.add).then_inc(x1_ready, 1)

            def normalise(j):
                dve.wait_ge(rstd_ready, j + 1)
                at_least(dve, hT_done, j)
                dve.tensor_scalar(h[:, :], ring_row(j, 0, D), mv1[:, 0:1], rstd1[:, :],
                                  ALU.subtract, ALU.mult).then_inc(h_ready, 1)

            def h_low(j):
                dve.wait_ge(hT_hi_done, j + 1)
                dve.tensor_tensor(hT_lo[:, :, :].rearrange("p k t -> p (k t)"), hT_ps[:, :],
                                  hT_hi[:, :, :].rearrange("p k t -> p (k t)").bitcast(FP32),
                                  ALU.subtract).then_inc(hT_lo_done, 1)

            def a_low(j, bank=aT_ps, hi=aT_hi, lo=aT_lo):
                dve.wait_ge(aT_hi_done, j + 1)
                dve.tensor_tensor(lo[:, :, :].rearrange("p k t -> p (k t)"), bank[:, :],
                                  hi[:, :, :].rearrange("p k t -> p (k t)").bitcast(FP32),
                                  ALU.subtract).then_inc(aT_lo_done, 1)

            def up(j):
                dve.wait_ge(silu_done, j + 1)
                dve.tensor_tensor(a[:, :], z_ps[:, :], a[:, :], ALU.mult).then_inc(a_ready, 1)

            for n in range(BY_ACT, E * KD):
                if n == 8:
                    rows_statistics(0)
                if n == 10:
                    normalise(0)
                if n == 12:
                    rows_statistics(1)
                dve.wait_ge(ctx_hi_done, n + 1)
                dve.tensor_tensor(ctx_lo[:, n * F1:(n + 1) * F1], o_ps[n % 4][:, :],
                                  ctx_hi[:, n * F1:(n + 1) * F1].bitcast(FP32), ALU.subtract).then_inc(ctx_lo_done, 1)
            dve.wait_ge(tg_done, 1)
            h_low(0)
            normalise(1)
            dve.wait_ge(gwT_done, 1)
            dve.tensor_copy(gwT[:, :, :], y_ps[:, 0:KD * NE].rearrange("p (k e) -> p k e", e=NE)).then_inc(gwT_copied, 1)
            for c in range(FC):
                dve.tensor_copy(b1T[0:FM[c], c, :], y_ps[0:FM[c], (KD + c) * NE:(KD + c + 1) * NE]).then_inc(gwT_copied, 1)
            up(0)
            h_low(1)
            rows_statistics(2)
            dve.memset(act_last[:, :], 1.0).then_inc(pads_made, 1)
            a_low(0)
            normalise(2)
            h_low(2)
            up(1)
            rows_statistics(3)
            STEPS = 4
            steps = chain.at
            with dve.Fori(2, PREP) as j:
                chain.at = steps + (j - 2) * STEPS
                a_low(j - 1)
                normalise(j + 1)
                residual(j - 2)
                h_low(j + 1)
                up(j)
                rows_statistics(j + 2)
            chain.at = steps + (PREP - 2) * STEPS
            def ffn_normalise(b, ts=range(TT)):
                at_least(dve, h2T_done, KD * b)
                for t in ts:
                    dve.wait_ge(x1_here[t], 16 * b + 16)
                    at = (b % 2) * X1B + t * DS
                    dve.tensor_scalar(h2[:, t * D:(t + 1) * D], x1b[:, bass.ds(at, D)], x1b[:, bass.ds(at + D, 1)],
                                      x1b[:, bass.ds(at + D + 1, 1)], ALU.subtract, ALU.mult).then_inc(h2_ready, 1)

            def ffn_h_low(b, banks):
                for k in range(KD):
                    dve.wait_ge(h2T_hi_done, KD * b + k + 1)
                    place = bass.ds((b % 2) * (KD * S) + k * S, S)
                    dve.tensor_tensor(h2T_lo[:, place], banks[k % len(banks)][:, :], h2T_hi[:, place].bitcast(FP32),
                                      ALU.subtract).then_inc(h2T_lo_done, 1)

            def scale_logits(b):
                dve.wait_ge(logit_done, b + 1)
                run(dve.tensor_scalar(logit[:, :], t_ps[0][0:1, 0:NE], 1.0 / S, None, ALU.mult))
                dve.tensor_reduce(neg_max[:, :], logit[:, :], AX_X, ALU.max, negate=True).then_inc(neg_max_ready, 1)

            def choose(b):
                dve.wait_ge(expo_done, b + 1)
                run(dve.reciprocal(einv[:, :], esum[:, :]))
                run(dve.tensor_scalar(prob[:, 0:NE], expo[:, :], einv[:, 0:1], None, ALU.mult), apart=True)
                run(dve.max(top[:, :], prob[:, :]), apart=True)
                dve.max_index(top_idx[:, :], top[:, :], prob[:, :]).then_inc(gate_ready, 1)
                run(dve.tensor_tensor(tsum[:, :], top[:, 0:1], top[:, 1:2], ALU.add))
                run(dve.reciprocal(tinv[:, :], tsum[:, :]))
                dve.tensor_scalar(mix1[:, :], top[:, 0:2], tinv[:, 0:1], tg[0:1, 1:2],
                                  ALU.mult, ALU.mult).then_inc(mix1_ready, 1)

            def spread_mix(b):
                dve.wait_ge(mix_spread, b + 1)
                dve.tensor_copy(mix[:, bass.ds((b % 2) * 2, 2)], t_ps[1][:, 0:2]).then_inc(mix_ready, 1)

            def split_low(b, s, piece):
                dve.wait_ge(hi_done[s], len(PARTS) * b + piece + 1)
                place = PARTS[piece]
                dve.tensor_tensor(w_lo[s][:, place], w_raw[s][:, place], w_hi[s][:, place].bitcast(FP32),
                                  ALU.subtract).then_inc(lo_done[s], 1)

            def weigh(b, s, c):
                dve.wait_ge(gelu_done, (2 * b + s) * FC + c + 2)
                wait_primed(dve, pair_done, 2 * b + s)
                if s == 0 and c == 0:
                    dve.wait_ge(mix_ready, b + 1)
                rows = P if c < FC - 1 else BIAS_ROW + 1
                src = act[0:rows, c % 2, :] if c < FC - 1 else act_last[0:rows, :]
                w = mix[0:rows, bass.ds((b % 2) * 2 + s, 1)]
                run(dve.tensor_scalar(a2_hi[0:rows, c, :], src, w, None, ALU.mult))
                dve.scalar_tensor_tensor(a2_lo[0:rows, c, :], src, w, a2_hi[0:rows, c, :].bitcast(FP32),
                                         ALU.mult, ALU.subtract).then_inc(a2_ready, 1)

            def finish(b):
                for t in range(TT):
                    dve.wait_ge(o_done, TT * b + t + 1)
                    place = x1b[:, bass.ds((b % 2) * X1B + t * DS, D)]
                    dve.tensor_tensor(place, o_ps[t][:, :], place, ALU.add).then_inc(o_taken, 1)

            for j in range(PREP, TILES):
                if j == PREP + 5:
                    spread_mix(0)
                a_low(j - 1)
                if j == PREP + 3:
                    scale_logits(0)
                if j + 1 < TILES:
                    normalise(j + 1)
                residual(j - 2)
                if j + 1 < TILES:
                    h_low(j + 1)
                up(j)
                if j + 2 < TILES:
                    rows_statistics(j + 2)
                if j < PREP + 2:
                    half_of_batch = TT // 2 * (j - PREP)
                    ffn_normalise(0, range(half_of_batch, half_of_batch + TT // 2))
                if j == PREP + 3:
                    choose(0)
                if j == PREP + 5:
                    split_low(0, 0, 0)
                    split_low(0, 0, 1)
            a_low(TILES - 1, hT_ps, hT_hi, hT_lo)
            residual(TILES - 2)
            ffn_h_low(0, o_ps)
            residual(TILES - 1, aT_ps)
            dve.wait_ge(pads_made, 4)
            split_low(0, 0, 2)
            steps = chain.at
            STEPS_OF_BATCH = 6 + 2 * FC

            def batch(b, more):
                for c in range(FC):
                    weigh(b, 0, c)
                    if c < 2:
                        split_low(b, 1, c)
                if more:
                    ffn_normalise(b + 1)
                split_low(b, 1, 2)
                if more:
                    ffn_h_low(b + 1, t_ps)
                    scale_logits(b + 1)
                    choose(b + 1)
                for c in range(FC):
                    weigh(b, 1, c)
                if more:
                    spread_mix(b + 1)
                    for piece in range(len(PARTS)):
                        split_low(b + 1, 0, piece)
                finish(b)

            with dve.Fori(0, B - 1) as b:
                chain.at = steps + b * STEPS_OF_BATCH
                batch(b, True)
            chain.at = steps + (B - 1) * STEPS_OF_BATCH
            batch(B - 1, False)

        @block.scalar
        def _(sc):
            sc.dma_start(gates_in[:, 0:1], g_xattn.rearrange("(o n) -> o n", o=1)).then_inc(gates_here, 16)
            sc.dma_start(gates_in[:, 1:2], g_ffn.rearrange("(o n) -> o n", o=1)).then_inc(gates_here, 16)
            sc.dma_start(gw_rows[:, :], gate_w).then_inc(gw_here, 16)
            sc.dma_start(b1_rows[:, :], b1).then_inc(gw_here, 16)
            def h_high(j):
                sc.wait_ge(hT_done, j + 1)
                at_least(sc, z_done, j)
                sc.activation(hT_hi[:, :, :].rearrange("p k t -> p (k t)"), hT_ps[:, :], ACT.Copy).then_inc(hT_hi_done, 1)

            def a_high(j):
                sc.wait_ge(aT_done, j + 1)
                at_least(sc, y_done, j)
                sc.activation(aT_hi[:, :, :].rearrange("p k t -> p (k t)"), aT_ps[:, :], ACT.Copy).then_inc(aT_hi_done, 1)

            def silu_of(j):
                sc.wait_ge(z_done, j + 1)
                sc.activation(a[:, :], z_ps[:, :], ACT.Silu).then_inc(silu_done, 1)

            warming = Chain(sc, warmed, waited)

            def bring_tables(function):
                warming.run(sc.activation(warm[:, :], tg[0:1, :], function))

            def split_low_alone(n):
                sc.wait_ge(ctx_rest_done, n + 1)
                sc.activation(ctx_lo[:, n * F1:(n + 1) * F1], o_ps[n % 4][:, :], ACT.Copy).then_inc(ctx_lo_by_act, 1)

            for n in range(E * KD):
                sc.wait_ge(ctxT_done, n + 1)
                sc.activation(ctx_hi[:, n * F1:(n + 1) * F1], o_ps[n % 4][:, :], ACT.Copy).then_inc(ctx_hi_done, 1)
                if 1 <= n <= BY_ACT:
                    split_low_alone(n - 1)
                if n == 11:
                    sc.wait_ge(tanh_in, 1)
                    sc.activation(tg[:, :], z_ps[:, 0:2], ACT.Tanh).then_inc(tg_done, 1)
                    sc.wait_ge(tg_done, 1)
                    bring_tables(ACT.Silu)

            h_high(0)
            silu_of(0)
            h_high(1)
            a_high(0)
            silu_of(1)
            h_high(2)
            with sc.Fori(2, PREP) as j:
                a_high(j - 1)
                silu_of(j)
                h_high(j + 1)
            def ffn_h_high(b, banks):
                for k in range(KD):
                    sc.wait_ge(h2T_done, KD * b + k + 1)
                    sc.activation(h2T_hi[:, bass.ds((b % 2) * (KD * S) + k * S, S)], banks[k % len(banks)][:, :],
                                  ACT.Identity, accum_out=hsum[:, k:k + 1]).then_inc(h2T_hi_done, 1)

            def token_sums():
                for k in range(KD):
                    sc.wait_ge(h2T_done, k + 1)
                    sc.activation(x1b[:, X1B + k * S:X1B + (k + 1) * S], o_ps[k][:, :], ACT.Identity,
                                  accum_out=hsum[:, k:k + 1]).then_inc(sums_done, 1)

            def exponents(b):
                sc.wait_ge(neg_max_ready, b + 1)
                sc.activation(expo[:, :], logit[:, :], ACT.Exp, bias=neg_max[:, 0:1],
                              accum_out=esum[:, 0:1]).then_inc(expo_done, 1)

            def split_high(b, s, piece):
                here, each = ((w1_here[s], 16), (w1_rest_here[s], 16), (w2_here[s], 16 * W2_DMAS))[piece]
                sc.wait_ge(here, each * (b + 1))
                if not (isinstance(b, int) and b == 0 and s == 0):
                    wait_primed(sc, pair_done, 2 * b + s - 1)
                place = PARTS[piece]
                sc.activation(w_hi[s][:, place], w_raw[s][:, place], ACT.Copy).then_inc(hi_done[s], 1)

            def gelu_of(b, s, c, e):
                k = s * FC + c
                sc.wait_ge(hid_done, 2 * FC * b + k + 1)
                rows = FM[c]
                dst = act[:, c % 2, :] if c < FC - 1 else act_last[0:rows, :]
                wait_primed(sc, a2_ready, 2 * FC * b + max(k - FC + 1, 0))
                sc.activation(dst, hid_ps[k % 2][0:rows, :], ACT.Gelu, bias=b1T[0:rows, c, bass.ds(e, 1)]).then_inc(gelu_done, 1)

            for j in range(PREP, TILES):
                a_high(j - 1)
                silu_of(j)
                if j + 1 < TILES:
                    h_high(j + 1)
                if j == PREP + 2:
                    token_sums()
                if j == PREP + 3:
                    exponents(0)
                    bring_tables(ACT.Silu)
                if j == PREP + 5:
                    split_high(0, 0, 0)
                    split_high(0, 0, 1)
            sc.wait_ge(aT_done, TILES)
            sc.activation(hT_hi[:, :, :].rearrange("p k t -> p (k t)"), hT_ps[:, :], ACT.Copy).then_inc(aT_hi_done, 1)
            split_high(0, 0, 2)
            sc.wait_ge(y_done, TILES)
            ffn_h_high(0, o_ps)
            sc.wait_ge(gwT_copied, 1 + FC)

            def batch(b, more):
                bring_tables(ACT.Gelu)
                wait_apart(sc, gate_ready, b + 1, waited)
                chosen = [sc.value_load(top_idx[0:1, s:s + 1], min_val=0, max_val=NE - 1) for s in range(2)]
                gelu_of(b, 0, 0, chosen[0])
                split_high(b, 1, 0)
                split_high(b, 1, 1)
                gelu_of(b, 0, 1, chosen[0])
                split_high(b, 1, 2)
                for c in range(2, FC):
                    gelu_of(b, 0, c, chosen[0])
                if more:
                    ffn_h_high(b + 1, t_ps)
                    bring_tables(ACT.Exp)
                    exponents(b + 1)
                    bring_tables(ACT.Gelu)
                for c in range(FC):
                    gelu_of(b, 1, c, chosen[1])
                if more:
                    for piece in range(len(PARTS)):
                        split_high(b + 1, 0, piece)

            warm_before = warming.at
            WARMED_IN_BATCH = 3
            with sc.Fori(0, B - 1) as b:
                warming.at = warm_before + b * WARMED_IN_BATCH
                batch(b, True)
            warming.at = warm_before + (B - 1) * WARMED_IN_BATCH
            batch(B - 1, False)

        @block.tensor
        def _(pe):
            pe.wait_ge(consts_made, 4)
            pe.wait_ge(ones_made, 2)
            pe.wait_ge(rowcnt_done, 1)
            pe.matmul(hT_ps[:, 0:E], below[:, :], rowcnt[:, :], start=True, stop=True)
            pe.matmul(hT_ps[:, E:2 * E], early[:, :], rowcnt[:, :], start=True, stop=True)
            pe.matmul(hT_ps[:, 2 * E:3 * E], ones_h[:, :], rowcnt[:, :], start=True, stop=True).then_inc(counts_done, 1)

            def turn_small_tables():
                pe.wait_ge(gates_here, 32)
                pe.matmul(z_ps[:, 0:2], ones[0:1, :], gates_in[0:1, :], start=True, stop=True).then_inc(tanh_in, 1)
                pe.wait_ge(gw_here, 32)
                for k in range(KD):
                    pe.transpose(y_ps[:, k * NE:(k + 1) * NE], gw_rows[:, k * P:(k + 1) * P], ident[0:NE, 0:NE])
                for c in range(FC):
                    last = pe.transpose(y_ps[0:FM[c], (KD + c) * NE:(KD + c + 1) * NE], b1_rows[:, c * P:c * P + FM[c]],
                                        ident[0:NE, 0:NE])
                last.then_inc(gwT_done, 1)

            def invert():
                pe.wait_ge(slot_hot_done, IDC)
                pe.wait_ge(tile_hot_done, 1)
                for c in range(IDC):
                    last = pe.matmul(aT_ps[:, 0:DIGITS * TILES], slot_hot[:, c, :],
                                     tile_hot[:, c].rearrange("p g j -> p (g j)"), start=(c == 0), stop=(c == IDC - 1))
                last.then_inc(rows_done, 1)

            def split_product(dst, stationary, moving, first, last):
                s_hi, s_lo = stationary
                m_hi, m_lo = moving
                pe.matmul(dst, s_hi, m_lo, start=first, stop=False)
                pe.matmul(dst, s_hi, m_hi, start=False, stop=False)
                return pe.matmul(dst, s_lo, m_hi, start=False, stop=last)

            def transpose_h(j):
                pe.wait_ge(h_ready, j + 1)
                at_least(pe, hT_lo_done, j)
                for k in range(KD):
                    last = pe.transpose(hT_ps[:, k * P:(k + 1) * P], h[:, k * P:(k + 1) * P], ident[:, :])
                last.then_inc(hT_done, 1)

            def transpose_a(j, bank=aT_ps):
                pe.wait_ge(a_ready, j + 1)
                at_least(pe, aT_lo_done, j)
                for k in range(KF1):
                    last = pe.transpose(bank[:, k * P:(k + 1) * P], a[:, k * P:(k + 1) * P], ident[:, :])
                last.then_inc(aT_done, 1)

            def expert_of(j):
                return pe.value_load(te_i[0:1, bass.ds(j, 1)], min_val=0, max_val=E - 1)

            def expert_product(e, dst, src_hi, src_lo, lo_done, count, first_wait=None, between=None):
                def product(k, src, weights, first, last):
                    return pe.matmul(dst[:, :], src[:, k, :], weights[:, bass.ds(e * (KD * F1) + k * F1, F1)],
                                     start=first, stop=last)

                for k in range(KD):
                    product(k, src_hi, ctx_hi, k == 0, False)
                if first_wait:
                    first_wait()
                for k in range(KD):
                    product(k, src_hi, ctx_lo, False, False)
                pe.wait_ge(lo_done, count)
                for k in range(KD):
                    if between and k == KD - 1:
                        between()
                    last = product(k, src_lo, ctx_hi, False, k == KD - 1)
                return last

            def first_product(j, e, first_wait=None):
                pe.wait_ge(hT_hi_done, j + 1)
                at_least(pe, a_ready, j)
                expert_product(e, z_ps, hT_hi, hT_lo, hT_lo_done, j + 1, first_wait).then_inc(z_done, 1)

            def second_product(j, e, between=None):
                pe.wait_ge(aT_hi_done, j + 1)
                at_least(pe, y_taken, j)
                expert_product(e, y_ps, aT_hi, aT_lo, aT_lo_done, j + 1, between=between).then_inc(y_done, 1)

            for n in range(E * KD):
                if n == 2:
                    invert()
                if n == 8:
                    turn_small_tables()
                e, k = divmod(n, KD)
                if k == 0:
                    pe.wait_ge(ctx_here[e], 16)
                if 4 <= n < 4 + BY_ACT:
                    pe.wait_ge(ctx_lo_by_act, n - 3)
                elif n >= 4:
                    pe.wait_ge(ctx_lo_done, n - 3 - BY_ACT)
                for m in range(KF1):
                    last = pe.transpose(o_ps[n % 4][:, m * P:(m + 1) * P], raw_ctx[:, e, m, k * P:(k + 1) * P], ident[:, :])
                last.then_inc(ctxT_done, 1)
                if 1 <= n <= BY_ACT:
                    pe.wait_ge(ctx_hi_done, n)
                    e, k = divmod(n - 1, KD)
                    for m in range(KF1):
                        pe.matmul(o_ps[(n - 1) % 4][:, m * P:(m + 1) * P], raw_ctx[:, e, m, k * P:(k + 1) * P],
                                  ident[:, :], is_transpose=True, start=(m == 0), stop=False)
                    pe.matmul(o_ps[(n - 1) % 4][:, :], neg_ident[:, :], ctx_hi[:, (n - 1) * F1:n * F1],
                              start=False, stop=True).then_inc(ctx_rest_done, 1)

            transpose_h(0)
            pe.wait_ge(routed, 2)
            e = expert_of(0)
            pe.wait_ge(ctx_hi_done, E * KD)

            def low_context():
                pe.wait_ge(ctx_lo_by_act, BY_ACT)
                pe.wait_ge(ctx_lo_done, E * KD - BY_ACT)

            first_product(0, e, low_context)
            transpose_h(1)

            def tile_step(j):
                e_before, e = expert_of(j - 1), expert_of(j)
                transpose_a(j - 1)
                first_product(j, e)
                transpose_h(j + 1)
                second_product(j - 1, e_before)

            tile_step(1)
            with pe.Fori(2, PREP) as j:
                tile_step(j)

            def transpose_h2(b, ks):
                pe.wait_ge(h2_ready, TT * b + TT)
                for k in ks:
                    if k == 1:
                        pe.wait_ge(mix_ready, b)
                    pe.wait_ge(h2T_lo_done, KD * b + max(k - 1, 0))
                    for t in range(TT):
                        last = pe.transpose(t_ps[k % 2][:, t * P:(t + 1) * P],
                                            h2[:, t * D + k * P:t * D + (k + 1) * P], ident[:, :])
                    last.then_inc(h2T_done, 1)

            def transpose_first_h2():
                pe.wait_ge(h2_ready, TT)
                for k in range(KD):
                    for t in range(TT):
                        last = pe.transpose(o_ps[k][:, t * P:(t + 1) * P],
                                            h2[:, t * D + k * P:t * D + (k + 1) * P], ident[:, :])
                    last.then_inc(h2T_done, 1)

            def logits(b):
                if isinstance(b, int) and b == 0:
                    pe.wait_ge(sums_done, KD)
                    pe.wait_ge(hT_lo_done, PREP + 4)
                else:
                    pe.wait_ge(h2T_hi_done, KD * b + KD)
                    pe.wait_ge(h2T_lo_done, KD * b + KD - 1)
                for k in range(KD):
                    last = pe.matmul(t_ps[0][0:1, 0:NE], hsum[:, k:k + 1], gwT[:, k, :], start=(k == 0), stop=(k == KD - 1))
                last.then_inc(logit_done, 1)

            def spread_mix(b):
                pe.wait_ge(mix1_ready, b + 1)
                pe.matmul(t_ps[1][:, 0:2], ones[0:1, :], mix1[:, :], start=True, stop=True).then_inc(mix_spread, 1)

            def hidden(b, s, between=None):
                for c in range(FC):
                    k6 = s * FC + c
                    wait_primed(pe, gelu_done, 2 * FC * b + max(k6 - 1, 0))
                    if c < 2:
                        pe.wait_ge(lo_done[s], len(PARTS) * b + c + 1)
                    for k in range(KD):
                        if c == 0:
                            pe.wait_ge(h2T_lo_done, KD * b + k + 1)
                        col0 = k * P if c == 0 else KD * P + k * (F2 - P) + (c - 1) * P
                        rows = bass.ds((b % 2) * (KD * S) + k * S, S)
                        last = split_product(hid_ps[k6 % 2][0:FM[c], :],
                                             (w_hi[s][:, col0:col0 + FM[c]], w_lo[s][:, col0:col0 + FM[c]]),
                                             (h2T_hi[:, rows], h2T_lo[:, rows]), k == 0, k == KD - 1)
                    last.then_inc(hid_done, 1)
                    if between and c == 0:
                        between(b + 1)

            def output(b, s, cs, ts=range(TT)):
                pe.wait_ge(lo_done[s], len(PARTS) * (b + 1))
                for c in cs:
                    pe.wait_ge(a2_ready, (2 * b + s) * FC + c + 2)
                if s == 0 and cs[0] == 0:
                    wait_primed(pe, o_taken, TT * b)
                for t in ts:
                    for c in cs:
                        rows = P if c < FC - 1 else BIAS_ROW + 1
                        place = slice(W1N + c * D, W1N + (c + 1) * D)
                        last = split_product(o_ps[t][:, :],
                                             (a2_hi[0:rows, c, t * P:(t + 1) * P], a2_lo[0:rows, c, t * P:(t + 1) * P]),
                                             (w_hi[s][0:rows, place], w_lo[s][0:rows, place]),
                                             s == 0 and c == 0, s == 1 and c == FC - 1)
                    if s == 1 and cs[-1] == FC - 1:
                        last.then_inc(o_done, 1)
                return last

            e_before, e = expert_of(PREP - 1), expert_of(PREP)
            for j in range(PREP, TILES):
                if j == PREP + 5:
                    pe.wait_ge(mix_ready, 1)
                transpose_a(j - 1)
                if j == PREP + 3:
                    logits(0)
                first_product(j, e)
                if j == PREP + 3:
                    pe.wait_ge(neg_max_ready, 1)
                if j + 1 < TILES:
                    transpose_h(j + 1)
                    if j == PREP + 2:
                        transpose_first_h2()
                    second_product(j - 1, e_before)
                    e_before, e = e, expert_of(j + 1)
                else:
                    second_product(j - 1, e_before, lambda: transpose_a(TILES - 1, hT_ps))
                if j == PREP + 4:
                    pe.wait_ge(aT_lo_done, PREP + 4)
                    spread_mix(0)
            pe.wait_ge(aT_hi_done, TILES)
            expert_product(e, aT_ps, hT_hi, hT_lo, aT_lo_done, TILES).then_inc(y_done, 1)
            pe.wait_ge(y_taken, TILES - 1)
            full = list(range(FC - 1))

            def batch(b, more):
                hidden(b, 0)
                output(b, 0, full)
                if more:
                    transpose_h2(b + 1, (0, 1))
                output(b, 0, [FC - 1], range(0, TT // 2))
                if more:
                    transpose_h2(b + 1, (2, 3))
                output(b, 0, [FC - 1], range(TT // 2, TT)).then_inc(pair_done, 1)
                if more:
                    logits(b + 1)
                hidden(b, 1, spread_mix if more else None)
                output(b, 1, full)
                output(b, 1, [FC - 1])
                pe.drain().then_inc(pair_done, 1)

            with pe.Fori(0, B - 1) as b:
                batch(b, True)
            batch(B - 1, False)


_INS = ["x", "itok_BxS_13_99985", "ctx_2048", "g_xattn", "g_ffn", "L0_ffn_gate_W", "L0_ffn_W1", "L0_ffn_b1",
        "L0_ffn_W2", "L0_ffn_b2"]


def kernel(**inputs):
    import numpy as _np
    import concourse.bacc as _bacc
    from concourse import mybir as _mybir
    from concourse.bass_utils import run_bass_kernel_spmd as _run

    nc = _bacc.Bacc("TRN2", target_bir_lowering=False, num_devices=1)
    arrays, args = {}, []
    for name in _INS:
        a = _np.ascontiguousarray(inputs[name])
        arrays[f"in_{name}"] = a
        args.append(nc.dram_tensor(f"in_{name}", a.shape, _mybir.dt.from_np(a.dtype), kind="ExternalInput").ap())
    shape = inputs["x"].shape
    args.append(nc.dram_tensor("out_0", shape, _mybir.dt.float32, kind="ExternalOutput").ap())
    flamingo_kernel(nc, *args)
    r = _run(nc, [arrays], core_ids=[0])
    return r.results[0]["out_0"]
```
